# Optimizing a Trainium2 kernel written in Bass

```python
import numpy as np
import jax
import jax.numpy as jnp

def _softmax(x, axis=-1):
    return jax.nn.softmax(x, axis=axis)

def _gelu(x):
    return jax.nn.gelu(x, approximate=True)

def _silu(x):
    return jax.nn.silu(x)

def _sigmoid(x):
    return jax.nn.sigmoid(x)

def _layernorm(x, axis=-1, eps=1e-05):
    m = jnp.mean(x, axis=axis, keepdims=True)
    v = jnp.var(x, axis=axis, keepdims=True)
    return (x - m) / jnp.sqrt(v + eps)

def _scatter_add(tgt, idx, src, axis=0):
    return tgt.at[idx].add(src)

def _segment_sum(src, seg, n):
    return jax.ops.segment_sum(src, seg, n)
kernel_name = 'mk_gnn_preln_d2_gnn_r32_9e51b2'

def setup_inputs(seed: int=0):
    np.random.seed(seed)
    _w = jnp.asarray

    def _rec_inputs():
        import jax
        import jax.numpy as jnp
        _gk = jax.random.key(seed)
        x = -0.0002117 + 1 * jax.random.normal(jax.random.fold_in(_gk, 1), (3125, 256), jnp.float32)
        _s = jax.random.randint(jax.random.fold_in(_gk, 2), (25000,), 0, 3125, jnp.int32)
        _d = jax.random.randint(jax.random.fold_in(_gk, 3), (25000,), 0, 3125, jnp.int32)
        _loop = jnp.arange(3125, dtype=jnp.int32)
        src = jnp.concatenate([_s, _d, _loop])
        dst = jnp.concatenate([_d, _s, _loop])
        _o = jnp.argsort(dst, stable=True)
        src = src[_o]
        dst = dst[_o]
        edge_attr_64 = 0.000279952 + 1.00013 * jax.random.normal(jax.random.fold_in(_gk, 11), (53125, 64), jnp.float32)
        edge_weight = jax.random.uniform(jax.random.fold_in(_gk, 13), (53125,), jnp.float32, 0.0, 1)
        return (x, src, dst, edge_attr_64, edge_weight)
    x, src, dst, edge_attr_64, edge_weight = _rec_inputs()

    def _L0_gnn_setup():
        import jax, jax.numpy as jnp
        import numpy as np
        N_NODES = 3125
        D = 256
        N_LAYERS = 3
        N_EDGES = 100000
        BN_EPS = 1e-05

        def _bn_train(x, gamma, beta):
            m = jnp.mean(x, axis=0)
            v = jnp.var(x, axis=0)
            return gamma * (x - m) * jax.lax.rsqrt(v + BN_EPS) + beta
        key = jax.random.key(seed)
        ks = jax.random.split(key, 16)
        s = 1.0 / np.sqrt(D)
        inp = {'x': jax.random.normal(ks[0], (N_NODES, D), dtype=jnp.float32), 'edge_index': jax.random.randint(ks[1], (2, N_EDGES), 0, N_NODES, dtype=jnp.int64 if jax.config.jax_enable_x64 else jnp.int32), 'edge_weight': jax.random.uniform(ks[2], (N_EDGES,), dtype=jnp.float32), 'W_in': jax.random.uniform(ks[3], (D, D), jnp.float32, -s, s), 'b_in': jax.random.uniform(ks[4], (D,), jnp.float32, -s, s), 'W1': jax.random.uniform(ks[5], (N_LAYERS, D, D), jnp.float32, -s, s), 'b1': jax.random.uniform(ks[6], (N_LAYERS, D), jnp.float32, -s, s), 'g1': jnp.ones((N_LAYERS, D), jnp.float32), 'be1': jnp.zeros((N_LAYERS, D), jnp.float32), 'W2': jax.random.uniform(ks[7], (N_LAYERS, D, D), jnp.float32, -s, s), 'b2': jax.random.uniform(ks[8], (N_LAYERS, D), jnp.float32, -s, s), 'g_out': jnp.ones((N_LAYERS, D), jnp.float32), 'b_out': jnp.zeros((N_LAYERS, D), jnp.float32)}
        return inp
    _L0_gnn_all = _L0_gnn_setup()
    _L0_gnn_in = {k: v for k, v in _L0_gnn_all.items() if k in ('W_in', 'b_in', 'W1', 'b1', 'g1', 'be1', 'W2', 'b2', 'g_out', 'b_out')}
    del _L0_gnn_all

    def _L1_gnn_setup():
        import jax, jax.numpy as jnp
        import numpy as np
        N = 3125
        E = 10000
        CIN = 256
        EDIM = 64
        EEMB = 256
        H = 1024
        LN_EPS = 1e-05

        def _ln(x, g, b):
            m = jnp.mean(x, axis=-1, keepdims=True)
            v = jnp.var(x, axis=-1, keepdims=True)
            return (x - m) * jax.lax.rsqrt(v + LN_EPS) * g + b
        key = jax.random.key(seed)
        ks = jax.random.split(key, 16)

        def w(k, i, o):
            return (jax.random.normal(k, (i, o), jnp.float32) / np.sqrt(i)).astype(jnp.float32)
        return {'x': jax.random.normal(ks[0], (N, CIN), jnp.float32), 'edge_index': jax.random.randint(ks[1], (2, E), 0, N, dtype=jnp.int64), 'edge_attr': jax.random.normal(ks[2], (E, EDIM), jnp.float32), 'eps': jnp.float32(0.0), 'ee_w1': w(ks[3], EDIM, EEMB), 'ee_b1': jnp.zeros((EEMB,), jnp.float32), 'ee_w2': w(ks[4], EEMB, CIN), 'ee_b2': jnp.zeros((CIN,), jnp.float32), 'w1': w(ks[5], CIN, H), 'b1': jnp.zeros((H,), jnp.float32), 'g1': jnp.ones((H,), jnp.float32), 'be1': jnp.zeros((H,), jnp.float32), 'w2': w(ks[6], H, H), 'b2': jnp.zeros((H,), jnp.float32), 'g2': jnp.ones((H,), jnp.float32), 'be2': jnp.zeros((H,), jnp.float32), 'w3': w(ks[7], H, CIN), 'b3': jnp.zeros((CIN,), jnp.float32), 'bn_g': jnp.ones((CIN,), jnp.float32), 'bn_b': jnp.zeros((CIN,), jnp.float32)}
    _L1_gnn_all = _L1_gnn_setup()
    _L1_gnn_in = {k: v for k, v in _L1_gnn_all.items() if k in ('eps', 'ee_w1', 'ee_b1', 'ee_w2', 'ee_b2', 'w1', 'b1', 'g1', 'be1', 'w2', 'b2', 'g2', 'be2', 'w3', 'b3', 'bn_g', 'bn_b')}
    del _L1_gnn_all
    return {'x': x, 'src': src, 'dst': dst, 'edge_attr_64': edge_attr_64, 'edge_weight': edge_weight, 'L0_gnn_W_in': _L0_gnn_in['W_in'], 'L0_gnn_b_in': _L0_gnn_in['b_in'], 'L0_gnn_W1': _L0_gnn_in['W1'], 'L0_gnn_b1': _L0_gnn_in['b1'], 'L0_gnn_g1': _L0_gnn_in['g1'], 'L0_gnn_be1': _L0_gnn_in['be1'], 'L0_gnn_W2': _L0_gnn_in['W2'], 'L0_gnn_b2': _L0_gnn_in['b2'], 'L0_gnn_g_out': _L0_gnn_in['g_out'], 'L0_gnn_b_out': _L0_gnn_in['b_out'], 'L1_gnn_eps': _L1_gnn_in['eps'], 'L1_gnn_ee_w1': _L1_gnn_in['ee_w1'], 'L1_gnn_ee_b1': _L1_gnn_in['ee_b1'], 'L1_gnn_ee_w2': _L1_gnn_in['ee_w2'], 'L1_gnn_ee_b2': _L1_gnn_in['ee_b2'], 'L1_gnn_w1': _L1_gnn_in['w1'], 'L1_gnn_b1': _L1_gnn_in['b1'], 'L1_gnn_g1': _L1_gnn_in['g1'], 'L1_gnn_be1': _L1_gnn_in['be1'], 'L1_gnn_w2': _L1_gnn_in['w2'], 'L1_gnn_b2': _L1_gnn_in['b2'], 'L1_gnn_g2': _L1_gnn_in['g2'], 'L1_gnn_be2': _L1_gnn_in['be2'], 'L1_gnn_w3': _L1_gnn_in['w3'], 'L1_gnn_b3': _L1_gnn_in['b3'], 'L1_gnn_bn_g': _L1_gnn_in['bn_g'], 'L1_gnn_bn_b': _L1_gnn_in['bn_b']}

def reference(x, src, dst, edge_attr_64, edge_weight, L0_gnn_W_in, L0_gnn_b_in, L0_gnn_W1, L0_gnn_b1, L0_gnn_g1, L0_gnn_be1, L0_gnn_W2, L0_gnn_b2, L0_gnn_g_out, L0_gnn_b_out, L1_gnn_eps, L1_gnn_ee_w1, L1_gnn_ee_b1, L1_gnn_ee_w2, L1_gnn_ee_b2, L1_gnn_w1, L1_gnn_b1, L1_gnn_g1, L1_gnn_be1, L1_gnn_w2, L1_gnn_b2, L1_gnn_g2, L1_gnn_be2, L1_gnn_w3, L1_gnn_b3, L1_gnn_bn_g, L1_gnn_bn_b):
    import jax
    import jax.numpy as jnp

    def _L0_gnn_ref(x, edge_index, edge_weight, W_in, b_in, W1, b1, g1, be1, W2, b2, g_out, b_out):
        import jax, jax.numpy as jnp
        import numpy as np
        N_NODES = 3125
        D = 256
        N_LAYERS = 3
        N_EDGES = 100000
        BN_EPS = 1e-05

        def _bn_train(x, gamma, beta):
            m = jnp.mean(x, axis=0)
            v = jnp.var(x, axis=0)
            return gamma * (x - m) * jax.lax.rsqrt(v + BN_EPS) + beta
        row, col = (edge_index[0], edge_index[1])
        h = x @ W_in + b_in
        for l in range(N_LAYERS):
            msgs = edge_weight[:, None] * h[col]
            pooled = jax.ops.segment_sum(msgs, row, num_segments=N_NODES) + h
            hid = jax.nn.relu(_bn_train(pooled @ W1[l] + b1[l], g1[l], be1[l]))
            rep = hid @ W2[l] + b2[l]
            h = jax.nn.relu(_bn_train(rep, g_out[l], b_out[l]))
        return h

    def _L1_gnn_ref(x, edge_index, edge_attr, eps, ee_w1, ee_b1, ee_w2, ee_b2, w1, b1, g1, be1, w2, b2, g2, be2, w3, b3, bn_g, bn_b):
        import jax, jax.numpy as jnp
        import numpy as np
        N = 3125
        E = 10000
        CIN = 256
        EDIM = 64
        EEMB = 256
        H = 1024
        LN_EPS = 1e-05

        def _ln(x, g, b):
            m = jnp.mean(x, axis=-1, keepdims=True)
            v = jnp.var(x, axis=-1, keepdims=True)
            return (x - m) * jax.lax.rsqrt(v + LN_EPS) * g + b
        n = x.shape[0]
        sl = jnp.arange(n, dtype=edge_index.dtype)
        ei = jnp.concatenate([edge_index, jnp.stack([sl, sl], axis=0)], axis=1)
        ea = jnp.concatenate([edge_attr, jnp.zeros((n, edge_attr.shape[1]), edge_attr.dtype)], axis=0)
        src, dst = (ei[0], ei[1])
        e = jax.nn.relu(ea @ ee_w1 + ee_b1) @ ee_w2 + ee_b2
        msg = x[src] + e
        agg = jax.ops.segment_sum(msg, dst, num_segments=n)
        h = (1.0 + eps) * x + agg
        h = jax.nn.relu(_ln(h @ w1 + b1, g1, be1))
        h = jax.nn.relu(_ln(h @ w2 + b2, g2, be2))
        y = h @ w3 + b3
        out = x + y
        out = _ln(out, bn_g, bn_b)
        return jax.nn.relu(out)
    edge_index = jnp.stack([src, dst])
    h = jnp.maximum(_layernorm(x, axis=-1), 0.0)
    x = x + _L0_gnn_ref(h, edge_index, edge_weight, L0_gnn_W_in, L0_gnn_b_in, L0_gnn_W1, L0_gnn_b1, L0_gnn_g1, L0_gnn_be1, L0_gnn_W2, L0_gnn_b2, L0_gnn_g_out, L0_gnn_b_out)
    h = jnp.maximum(_layernorm(x, axis=-1), 0.0)
    x = x + _L1_gnn_ref(h, edge_index, edge_attr_64, L1_gnn_eps, L1_gnn_ee_w1, L1_gnn_ee_b1, L1_gnn_ee_w2, L1_gnn_ee_b2, L1_gnn_w1, L1_gnn_b1, L1_gnn_g1, L1_gnn_be1, L1_gnn_w2, L1_gnn_b2, L1_gnn_g2, L1_gnn_be2, L1_gnn_w3, L1_gnn_b3, L1_gnn_bn_g, L1_gnn_bn_b)
    return x

_drawn_inputs = setup_inputs


def setup_inputs(seed=0):
    import zlib

    import numpy as np

    out = dict(_drawn_inputs(seed))
    spreads = {'L0_gnn_g1': (1.0, 0.2),
     'L0_gnn_be1': (0.0, 0.1),
     'L0_gnn_g_out': (1.0, 0.2),
     'L0_gnn_b_out': (0.0, 0.1),
     'L1_gnn_ee_b1': (0.0, 0.394),
     'L1_gnn_ee_b2': (0.0, 0.1),
     'L1_gnn_b1': (0.0, 2.0),
     'L1_gnn_g1': (1.0, 0.2),
     'L1_gnn_be1': (0.0, 0.333),
     'L1_gnn_b2': (0.0, 0.1),
     'L1_gnn_g2': (1.0, 0.2),
     'L1_gnn_be2': (0.0, 0.307),
     'L1_gnn_b3': (0.0, 0.1),
     'L1_gnn_bn_g': (1.0, 0.2),
     'L1_gnn_bn_b': (0.0, 0.1)}
    factors = {'L0_gnn_b1': 64.0, 'L0_gnn_b2': 64.0}
    for name, (base, spread) in spreads.items():
        noise = np.random.default_rng([zlib.crc32(name.encode()), seed]).standard_normal(out[name].shape)
        drawn = base * np.exp(spread * noise) if base else spread * noise
        out[name] = jnp.asarray(drawn.astype(out[name].dtype))
    for name, factor in factors.items():
        out[name] = (out[name] * factor).astype(out[name].dtype)
    return out
```

```python
from contextlib import ExitStack

import concourse.bass as bass
from concourse import mybir

F32 = mybir.dt.float32
BF16 = mybir.dt.bfloat16
I32 = mybir.dt.int32
ALU = mybir.AluOpType
ACT = mybir.ActivationFunctionType
AX = mybir.AxisListType
ds = bass.ds

P = 128
N = 3125
D = 256
DH = D // P
NB = -(-N // P)
NP = NB * P
LASTR = N - (NB - 1) * P
E = 53125
EP = 125
ET = E // EP
CH = 4
TC = -(-ET // CH)
ETP = CH * TC
NBP = NB + 1
EA = 64
REC = 68
H = 5
RING = 2 * H
NT = -(-(E + NB * (P - 1)) // P)
NT = -(-NT // RING) * RING
NI = NT // RING
SC = 25
SCA = 13
G = 5
NG = NB // G
GC = G * P
HC = GC // 2
L = 3
HID = 1024
KH = HID // P
EPS = 1e-5
assert EP * ET == E and ET % SC == 0 and NB == G * NG


def build(nc, t, out):
    with ExitStack() as ctx:
        def sb(name, shape, dt=F32):
            return ctx.enter_context(nc.sbuf_tensor(name, shape, dt))

        def ps(name, shape, dt=F32):
            return ctx.enter_context(nc.psum_tensor(name, shape, dt))

        def sem(name):
            return ctx.enter_context(nc.semaphore(name))

        table = nc.dram_tensor("table", [NP, D], F32, kind="Internal").ap()
        h1_rows = nc.dram_tensor("h1_rows", [NP, D], F32, kind="Internal").ap()
        rec1_d = nc.dram_tensor("rec1_d", [P * NT, 4], F32, kind="Internal").ap()
        rec2_d = nc.dram_tensor("rec2_d", [P * NT, REC], F32, kind="Internal").ap()

        accT = sb("accT", [P, 4, NP])
        x_nm = sb("x_nm", [P, NB, D])
        rec1 = sb("rec1", [P, NT, 4])
        work = sb("work", [P, RING * (D + P) + DH * GC])
        ring = work[:, 0:RING * D].rearrange("p (j f) -> p j f", f=D)
        hot = work[:, RING * D:RING * (D + P)].rearrange("p (j f) -> p j f", f=P)
        stT = work[:, RING * (D + P):].rearrange("p (m c) -> p m c", m=DH)
        stF = work[:, RING * (D + P):]
        stR = stF.rearrange("p (b f) -> p b f", f=D)
        mlp = work[:, 0:4 * HID]
        stN = sb("stN", [P, G, D])
        W_in = sb("W_in", [P, DH, D])
        W1 = sb("W1", [P, L, DH, D])
        W2 = sb("W2", [P, L, DH, D])
        ee2 = sb("ee2", [P, DH, D])
        ee1 = sb("ee1", [EA + 1, D])
        region = sb("region", [P, HID * DH + HID * KH + D * KH])
        w1 = region[:, 0:HID * DH].rearrange("p (k n) -> p k n", k=DH)
        w2 = region[:, HID * DH:HID * (DH + KH)].rearrange("p (k n) -> p k n", k=KH)
        w3 = region[:, HID * (DH + KH):].rearrange("p (k n) -> p k n", k=KH)
        cur = [0]

        def carve(parts, cols, dt=F32):
            w = cols if dt != BF16 else -(-cols // 2)
            a = region[0:parts, cur[0]:cur[0] + w]
            cur[0] += w
            assert cur[0] <= region.shape[1]
            return a if dt == F32 else a.bitcast(dt)

        cur2 = [0]

        def carve2(parts, cols, dt=F32):
            w = cols if dt != BF16 else -(-cols // 2)
            a = ring[:, :, :].rearrange("p j f -> p (j f)")[0:parts, cur2[0]:cur2[0] + w]
            cur2[0] += w
            assert cur2[0] <= RING * D
            return a if dt == F32 else a.bitcast(dt)

        OH = carve(EP, NBP * ETP, BF16).rearrange("p (b t) -> p b t", b=NBP)
        srci = carve(EP, ETP, I32)
        dsti = carve(EP, ETP, I32)
        wgt = carve(EP, ETP)
        keyi = carve(EP, ETP, I32)
        keyf = carve(EP, ETP)
        loci = carve(EP, ETP, I32)
        locf = [carve(EP, ETP) for _ in range(2)]
        posf = carve(EP, ETP)
        term = carve(EP, ETP)
        pos = [carve(EP, ETP, I32) for _ in range(2)]
        low = carve(EP, ETP, I32)
        tot = carve2(TC, 2 * CH * EP, BF16).rearrange("p (r c m) -> p r c m", r=2, c=CH)
        U = carve2(TC, CH * ETP, BF16).rearrange("p (c t) -> p c t", c=CH)
        Lm = carve(EP, EP + 1, BF16)[:, 0:EP]
        onesb = carve(EP, EP + 1, BF16)[:, 0:EP]
        blk128 = carve2(NBP, NT)
        ended = carve2(NBP, NT)
        cnt = sb("cnt", [EP, NBP])
        padi = sb("padi", [NBP, P], I32)
        padf = sb("padf", [NBP, P])
        start = sb("start", [P, NBP])
        end = sb("end", [NBP, 1])
        U25 = sb("U25", [NBP, NBP])
        V25 = sb("V25", [NBP, NBP])
        blkoff = [sb(f"blkoff{s}", [1, NT], I32) for s in range(2)]
        fill1 = sb("fill1", [P, 44, 4])
        rr1 = sb("rr1", [EP, SC, 4])
        rr2 = sb("rr2", [EP, SC, REC])
        ridx = sb("ridx", [EP, SC], I32)
        gidx = sb("gidx", [P, RING], I32)
        chunk = sb("chunk", [P, 2, H, REC])
        fill2 = chunk[:, :, :, :].rearrange("p a j f -> p (a j) f")
        aT = sb("aT", [EA + 1, 2, P])
        emb = sb("emb", [P, 2, D])
        iota = sb("iota", [P, P])
        ident = sb("ident", [P, P])
        onesf = sb("onesf", [P, P])
        epsc = sb("epsc", [P, 1])
        st = sb("st", [P, NB, 6])
        mv = sb("mv", [P, NB, 2])
        sd = sb("sd", [P, NB])
        rs = sb("rs", [P, NB])
        nb = sb("nb", [P, NB])
        bst = sb("bst", [P, DH, 2 * NG, 6])
        bmv = sb("bmv", [P, DH, 2])
        bsd = sb("bsd", [P, DH])
        brs = sb("brs", [P, DH])
        bsc = sb("bsc", [P, DH])
        bms = sb("bms", [P, DH])
        bbi = sb("bbi", [P, DH])
        COLS = [("L0_gnn_b_in", 1)] + [(f"L0_gnn_{n}", L) for n in ("b1", "g1", "be1", "b2", "g_out", "b_out")] + \
               [("L1_gnn_ee_b1", 1), ("L1_gnn_ee_b2", 1)]
        vec = {n: sb("v_" + n, [P, k * DH]) for n, k in COLS}
        mvec = {n: sb("v_" + n, [P, KH]) for n in ("L1_gnn_g1", "L1_gnn_be1", "L1_gnn_g2", "L1_gnn_be2")}
        rows = {n: sb("r_" + n, [P, k]) for n, k in (("L1_gnn_b1", HID), ("L1_gnn_b2", HID), ("L1_gnn_b3", D),
                                                     ("L1_gnn_bn_g", D), ("L1_gnn_bn_b", D), ("L1_gnn_ee_b2", D))}
        epsv = sb("epsv", [P, 1])
        eps2 = sb("eps2", [P, 1])
        hblk = sb("hblk", [P, DH, P])
        z = [mlp[:, s * HID:s * HID + HID] for s in range(2)]
        zT = [mlp[:, (2 + s) * HID:(3 + s) * HID].rearrange("p (k n) -> p k n", k=KH) for s in range(2)]
        mst = [sb(f"mst{s}", [P, 2, 6]) for s in range(2)]
        mmv = [sb(f"mmv{s}", [P, 2]) for s in range(2)]
        msd = [sb(f"msd{s}", [P, 1]) for s in range(2)]
        mrs = [sb(f"mrs{s}", [P, 1]) for s in range(2)]
        mnb = [sb(f"mnb{s}", [P, 1]) for s in range(2)]
        h1b = stN[:, 0, :]
        y = stN[:, 1, :]
        yst = sb("yst", [P, 6])
        ymv = sb("ymv", [P, 2])
        ysd = sb("ysd", [P, 1])
        yrs = sb("yrs", [P, 1])
        ynb = sb("ynb", [P, 1])

        bank = [ps(f"bank{i}", [P, 512]) for i in range(8)]

        names = """keys_done edges_in x_in fills filled1 filled2 w_in vec_in scat_a scat_b rec1_in blk_done wl1_in
            stN_done tab_done ln_act m_h1 agg_mm m_o m_out m_st consts rec1_filled idx_done
            dve_c acc_done cnt_done totb_done pad_done starts_done ended_done sort_pe_r
            sort_dve_r pos_done ln_dve tr_done ev_T self_done hot_done ev_done bn_stat bn_sd
            bn_dve init_done mm_done m_sd m_rs m_mm3 m_y aT_done emb_done sort_pe_t sort_act_t
            rec_act stT_free st_done app_done tr2_done r_done m_blk m_mm1 m_a1 m_mm2 m_a2
            attr_a attr_b g_a g_b ch_a ch_b m_z1 m_n1 m_t1 m_z2 m_n2 m_t2""".split()
        S = {n: sem(n) for n in names}
        block = ctx.enter_context(nc.Block())
        AG = 4
        CR = RING

        def dram_T(ap, k):
            return ap.rearrange("(k p) n -> p k n", p=P)

        @block.sync
        def _(sp):
            v = lambda n: t[n].rearrange("(p t) -> p t", p=EP)
            sp.wait_ge(S["keys_done"], 1)
            sp.dma_start(srci[:, 0:ET], v("src")).then_inc(S["edges_in"], 16)
            sp.dma_start(dsti[:, 0:ET], v("dst")).then_inc(S["edges_in"], 16)
            sp.dma_start(wgt[:, 0:ET], v("edge_weight")).then_inc(S["edges_in"], 16)
            sp.dma_start(x_nm[:, 0:NB - 1, :], t["x"][0:(NB - 1) * P, :].rearrange("(b p) f -> p b f", p=P)
                         ).then_inc(S["x_in"], 16)
            sp.dma_start(x_nm[0:LASTR, NB - 1, :], t["x"][(NB - 1) * P:N, :]).then_inc(S["x_in"], 16)
            sp.wait_ge(S["fills"], 1)
            for q in range(NT // 44):
                sp.dma_start(rec1_d.rearrange("(p t) f -> p t f", p=P)[:, q * 44:(q + 1) * 44, :], fill1[:, :, :]
                             ).then_inc(S["filled1"], 16)
            for q in range(NT // RING):
                sp.dma_start(rec2_d.rearrange("(p t) f -> p t f", p=P)[:, q * RING:(q + 1) * RING, :],
                             fill2[:, :, :]).then_inc(S["filled2"], 16)
            sp.dma_start(W_in[:, :, :], dram_T(t["L0_gnn_W_in"], DH)).then_inc(S["w_in"], 16)
            for l in range(L):
                sp.dma_start(W1[:, l, :, :], dram_T(t["L0_gnn_W1"][l], DH)).then_inc(S["w_in"], 16)
                sp.dma_start(W2[:, l, :, :], dram_T(t["L0_gnn_W2"][l], DH)).then_inc(S["w_in"], 16)
            sp.dma_start(ee2[:, :, :], dram_T(t["L1_gnn_ee_w2"], DH)).then_inc(S["w_in"], 16)
            sp.dma_start(ee1[0:EA, :], t["L1_gnn_ee_w1"]).then_inc(S["w_in"], 16)
            sp.dma_start(ee1[EA:EA + 1, :], t["L1_gnn_ee_b1"].rearrange("(a n) -> a n", a=1)).then_inc(S["w_in"], 16)
            for n, k in COLS:
                a = t[n] if k == 1 else t[n].rearrange("l f -> (l f)")
                sp.dma_start(vec[n][:, :], a.rearrange("(c p) -> p c", p=P), allow_slow_non_contiguous=True).then_inc(S["vec_in"], 16)
            for n in mvec:
                sp.dma_start(mvec[n][:, :], t[n].rearrange("(c p) -> p c", p=P), allow_slow_non_contiguous=True).then_inc(S["vec_in"], 16)
            for n in rows:
                sp.dma_start(rows[n][:, :], t[n].partition_broadcast(P)
                             ).then_inc(S["vec_in"], 16)
            sp.dma_start(epsv[:, :], t["L1_gnn_eps"].partition_broadcast(P)).then_inc(S["vec_in"], 16)
            av = t["edge_attr_64"].rearrange("(p t) f -> p t f", p=EP)
            sp.wait_ge(S["fills"], 2)
            for i0, n in ((0, 1), (1, ET // SC - 1)):
                with sp.Fori(i0, i0 + n) as i:
                    for h, (a, b) in enumerate(((0, SCA), (SCA, SC))):
                        if i0:
                            sp.wait_ge(S["scat_" + "ab"[h]], 16 * (b - a) * (ET // SC) + i * (16 * (b - a)))
                        sp.dma_start(rr2[:, a:b, 0:EA], av[:, ds(i * SC + a, b - a), :]).then_inc(S["attr_" + "ab"[h]], 16)
            sp.wait_ge(S["scat_a"], 16 * SCA * (ET // SC))
            sp.wait_ge(S["scat_b"], 16 * (SC - SCA) * (ET // SC))
            sp.dma_start(rec1[:, :, :], rec1_d.rearrange("(p t) f -> p t f", p=P)).then_inc(S["rec1_in"], 16)
            sp.wait_ge(S["scat_a"], 2 * 16 * SCA * (ET // SC))
            sp.wait_ge(S["scat_b"], 2 * 16 * (SC - SCA) * (ET // SC))
            sp.wait_ge(S["blk_done"], 2)
            sp.dma_start(w1, dram_T(t["L1_gnn_w1"], DH)).then_inc(S["wl1_in"], 16)
            sp.dma_start(w2, dram_T(t["L1_gnn_w2"], KH)).then_inc(S["wl1_in"], 16)
            sp.dma_start(w3, dram_T(t["L1_gnn_w3"], KH)).then_inc(S["wl1_in"], 16)
            tv = table.rearrange("(b p) f -> p b f", p=P)
            hv = h1_rows.rearrange("(b p) f -> p b f", p=P)
            for u in range(AG - 1):
                with sp.Fori(0, NG) as g:
                    sp.wait_ge(S["stN_done"], NG * u + 1 + g)
                    sp.dma_start(tv[:, ds(g * G, G), :], stN[:, :, :]).then_inc(S["tab_done"], 16)
            with sp.Fori(0, NG) as g:
                sp.wait_ge(S["ln_act"], NB + 2 + G + g * G)
                sp.dma_start(hv[:, ds(g * G, G), :], stR).then_inc(S["m_h1"], 16)
                sp.wait_ge(S["stN_done"], NG * (AG - 1) + 1 + g)
                sp.dma_start(tv[:, ds(g * G, G), :], stN[:, :, :]).then_inc(S["tab_done"], 16)
            rv = rec2_d.rearrange("(p t) f -> p t f", p=P)
            with sp.Fori(0, NI) as i:
                for h in range(2):
                    sp.wait_ge(S["agg_mm"], NT * (AG - 1) + H * h + H + i * RING)
                    sp.dma_start(chunk[:, h, :, :], rv[:, ds(i * RING + h * H, H), :]
                                 ).then_inc(S["ch_" + "ab"[h]], 16)
            sp.wait_ge(S["m_h1"], 16 * NG)
            with sp.Fori(0, NB - 1) as b:
                sp.wait_ge(S["m_o"], 3 + b * 3)
                sp.dma_start(h1b[:, :], h1_rows[ds(b * P, P), :]).then_inc(S["m_h1"], 16)
                sp.wait_ge(S["m_out"], b + 1)
                sp.dma_start(out[ds(b * P, P), :], y[:, :]).then_inc(S["m_st"], 16)
            b = NB - 1
            sp.wait_ge(S["m_o"], 3 + b * 3)
            sp.dma_start(h1b[:, :], h1_rows[ds(b * P, P), :]).then_inc(S["m_h1"], 16)
            sp.wait_ge(S["m_out"], b + 1)
            sp.dma_start(out[b * P:N, :], y[0:LASTR, :]).then_inc(S["m_st"], 16)
            sp.wait_ge(S["m_st"], 16 * NB)

        @block.gpsimd
        def _(pool):
            k = [0]

            def c(ins):
                k[0] += 1
                ins.then_inc(S["consts"], 1)
                pool.wait_ge(S["consts"], k[0])

            c(pool.iota(iota[:, :], [[1, P]], base=0, channel_multiplier=0, allow_small_or_imprecise_dtypes=True))
            c(pool.iota(blk128, [[P, NT]], base=0, channel_multiplier=0, allow_small_or_imprecise_dtypes=True))
            c(pool.memset(onesf[:, :], 1.0))
            c(pool.memset(onesb, 1.0))
            c(pool.memset(epsc[:, :], EPS))
            c(pool.affine_select(out=ident[:, :], in_=onesf[:, :], compare_op=ALU.is_equal, fill=0.0, base=0,
                                 pattern=[[1, P]], channel_multiplier=-1))
            c(pool.affine_select(out=Lm, in_=onesb, compare_op=ALU.is_gt, fill=0.0, base=0,
                                 pattern=[[1, EP]], channel_multiplier=-1))
            c(pool.memset(U, 1.0))
            c(pool.affine_select(out=U, in_=U, compare_op=ALU.is_gt, fill=0.0, base=0,
                                 pattern=[[-TC, CH], [1, ETP]], channel_multiplier=-1))
            c(pool.affine_select(out=U25[:, :], in_=onesf[0:NBP, 0:NBP], compare_op=ALU.is_gt, fill=0.0, base=0,
                                 pattern=[[1, NBP]], channel_multiplier=-1))
            c(pool.affine_select(out=V25[:, :], in_=onesf[0:NBP, 0:NBP], compare_op=ALU.is_ge, fill=0.0, base=0,
                                 pattern=[[1, NBP]], channel_multiplier=-1))
            for s, (filled, rec, rd) in enumerate((("filled1", rr1, rec1_d), ("filled2", rr2, rec2_d))):
                pool.wait_ge(S[filled], 16 * (NT // (44, RING)[s]))
                for i0, n in ((0, 1), (1, ET // SC - 1)):
                    with pool.Fori(i0, i0 + n) as i:
                        for h, (a, b) in enumerate(((0, SCA), (SCA, SC))):
                            pool.wait_ge(S["rec1_filled"], s * 2 * (ET // SC) + 1 + h + i * 2)
                            pool.nop(nofuse=True)
                            for j in range(a, b):
                                pool.indirect_dma_start(rd[:, :], bass.IndirectOffsetOnAxis(ap=ridx[:, j:j + 1], axis=0),
                                                        rec[:, j, 0:REC if s else 4], None
                                                        ).then_inc(S["scat_" + "ab"[h]], 16)
            pool.wait_ge(S["rec1_in"], 16)
            for a in range(AG):
                pool.wait_ge(S["tab_done"], 16 * NG * (a + 1) + 16)
                if a == AG - 1:
                    pool.wait_ge(S["scat_a"], 2 * 16 * SCA * (ET // SC))
                with pool.Fori(0, NI) as i:
                    for h in range(2):
                        pool.wait_ge(S["agg_mm"], NT * a + H * h + H + i * RING)
                        if a < AG - 1:
                            idx = rec1[:, ds(i * RING + h * H, H), 0]
                        else:
                            pool.wait_ge(S["ch_" + "ab"[h]], 16 + i * 16)
                            idx = chunk[:, h, :, EA + 2]
                        pool.nop(nofuse=True)
                        pool.tensor_copy(gidx[:, h * H:h * H + H], idx.bitcast(I32)).then_inc(S["idx_done"], 1)
                        pool.wait_ge(S["idx_done"], NI * 2 * a + h + 1 + i * 2)
                        pool.nop(nofuse=True)
                        for j in range(h * H, h * H + H):
                            pool.indirect_dma_start(ring[:, j, :], None, table[:, :],
                                                    bass.IndirectOffsetOnAxis(ap=gidx[:, j:j + 1], axis=0)
                                                    ).then_inc(S["g_" + "ab"[h]], 16)

        @block.vector
        def _(dve):
            k = [0]

            def c(ins):
                k[0] += 1
                ins.then_inc(S["dve_c"], 1)
                dve.wait_ge(S["dve_c"], k[0])

            dve.sem_inc(S["acc_done"], 2)
            dve.sem_inc(S["tab_done"], 16)
            c(dve.memset(x_nm[:, NB - 1, :], 0.0))
            c(dve.memset(srci, 0))
            c(dve.memset(dsti, 0))
            dve.memset(wgt, 0.0).then_inc(S["keys_done"], 1)
            c(dve.memset(fill1[:, :, :], 0.0))
            c(dve.memset(fill1[:, :, 1], -1.0))
            c(dve.memset(fill2[:, :, :], 0.0))
            dve.memset(fill2[:, :, EA + 1], -1.0).then_inc(S["fills"], 1)
            dve.wait_ge(S["fills"], 1)
            dve.memset(rr2[:, :, EA], 1.0).then_inc(S["fills"], 1)
            c(dve.memset(rr2[:, :, EA + 3], 0.0))
            c(dve.memset(rr1[:, :, 3], 0.0))
            dve.wait_ge(S["edges_in"], 48)
            dve.wait_ge(S["consts"], 11)
            for s, arr in enumerate((srci, dsti)):
                c(dve.tensor_scalar(keyi, arr, 7, None, ALU.arith_shift_right))
                c(dve.tensor_copy(keyf, keyi))
                c(dve.memset(keyf[:, ET:ETP], -1.0))
                c(dve.tensor_scalar(loci, arr, P - 1, None, ALU.bitwise_and))
                c(dve.tensor_copy(locf[s], loci))
                for b in range(NBP):
                    c(dve.tensor_scalar(OH[:, b, :], keyf, float(b), None, ALU.is_equal))
                dve.tensor_reduce(cnt[:, :], OH, AX.X, ALU.add).then_inc(S["cnt_done"], 1)
                dve.wait_ge(S["totb_done"], s + 1)
                c(dve.tensor_copy(padi[:, :], bank[0][0:NBP, 0:P]))
                c(dve.tensor_scalar(padi[:, :], padi[:, :], P - 1, None, ALU.add))
                c(dve.tensor_scalar(padi[:, :], padi[:, :], 7, None, ALU.arith_shift_right))
                dve.tensor_scalar(padf[:, :], padi[:, :], float(P), None, ALU.mult).then_inc(S["pad_done"], 1)
                dve.wait_ge(S["starts_done"], s + 1)
                c(dve.tensor_copy(start[:, :], bank[1][:, 0:NBP]))
                c(dve.tensor_copy(end[:, :], bank[2][0:NBP, 0:1]))
                dve.tensor_scalar(ended, blk128, end[:, 0:1], None, ALU.is_ge).then_inc(S["ended_done"], 1)
                dve.wait_ge(S["blk_done"], s + 1)
                c(dve.tensor_scalar(blkoff[s][:, :], bank[3][0:1, 0:NT], float(NB - 1), float(P), ALU.min, ALU.mult))
                c(dve.memset(posf, 0.0))
                for b in range(NBP):
                    dve.wait_ge(S["sort_pe_r"], NBP * s + b + 1)
                    dve.scalar_tensor_tensor(term, bank[6 + b % 2][0:EP, 0:ETP], start[0:EP, b:b + 1], OH[:, b, :],
                                             ALU.add, ALU.mult).then_inc(S["sort_dve_r"], 1)
                    dve.wait_ge(S["sort_dve_r"], NBP * s + b + 1)
                    c(dve.tensor_tensor(posf, posf, term, ALU.add))
                c(dve.tensor_copy(keyi, posf))
                c(dve.tensor_scalar(low, keyi, P - 1, None, ALU.bitwise_and))
                c(dve.tensor_scalar(keyi, keyi, 7, None, ALU.arith_shift_right))
                dve.scalar_tensor_tensor(pos[s], low, float(NT), keyi, ALU.mult, ALU.add).then_inc(S["pos_done"], 1)
                dve.wait_ge(S["pos_done"], s + 1)

            def row_stats(r):
                with dve.Fori(0, NG) as g:
                    for j in range(G):
                        dve.bn_stats(st[:, ds(g * G + j, 1), :], x_nm[:, ds(g * G + j, 1), :]).then_inc(S["ln_dve"], 1)
                dve.wait_ge(S["ln_dve"], (2 * r + 1) * NB + r)
                for b in range(NB):
                    dve.bn_aggr(mv[:, b, :], st[:, b, :]).then_inc(S["ln_dve"], 1)
                dve.wait_ge(S["ln_act"], r * (NB + 1) + 1)
                c(dve.reciprocal(rs[:, :], sd[:, :]))
                dve.scalar_tensor_tensor(nb[:, :], mv[:, :, 0], -1.0, rs[:, :], ALU.mult, ALU.mult
                                         ).then_inc(S["ln_dve"], 1)

            dve.wait_ge(S["x_in"], 32)
            row_stats(0)
            pT = [bank[4], bank[5]]
            with dve.Fori(0, NG) as g:
                for m in range(DH):
                    for hh in range(2):
                        n = 3 if hh == 0 else 2
                        dve.wait_ge(S["tr_done"], m * 2 + hh + 1 + g * 4)
                        dve.tensor_copy(accT[:, 2 + m, ds(g * GC + hh * 3 * P, n * P)], bank[4 + m * 2 + hh][:, 0:n * P]
                                        ).then_inc(S["ev_T"], 1)

            def rows_from_columns(u):
                with dve.Fori(0, NG) as g:
                    for q in range(3):
                        n = 2 if q < 2 else 1
                        dve.wait_ge(S["tr_done"], 4 * NG + u * 3 * NG + q + 1 + g * 3)
                        src = bank[4 + q][:, 0:n * D].rearrange("p (b f) -> p b f", f=D)
                        if u < AG - 1:
                            if q == 0:
                                dve.wait_ge(S["tab_done"], 16 * NG * u + 16 + g * 16)
                            ins = dve.tensor_copy(stN[:, 2 * q:2 * q + n, :], src)
                            ins.then_inc(S["ev_T"], 1)
                            if q == 2:
                                dve.wait_ge(S["ev_T"], 4 * NG + u * 3 * NG + 3 + g * 3)
                                dve.sem_inc(S["stN_done"], 1)
                        else:
                            xs = x_nm[:, ds(g * G + 2 * q, n), :]
                            dve.tensor_tensor(xs, xs, src, ALU.add).then_inc(S["ev_T"], 1)

            def accumulate(a):
                dve.wait_ge(S["self_done"], NG * (a + 1 + (a == AG - 1)))
                if a == 0:
                    dve.wait_ge(S["rec1_in"], 16)
                lastp = a == AG - 1
                with dve.Fori(0, NI) as i:
                    for h in range(2):
                        for j in range(h * H, h * H + H):
                            if j % H == 0:
                                dve.wait_ge(S["agg_mm"], NT * a + h * H + H + i * RING)
                                if lastp:
                                    dve.wait_ge(S["ch_" + "ab"[h]], 16 + i * 16)
                            if lastp:
                                ins = dve.tensor_scalar(hot[:, j, :], iota[:, :], chunk[:, h, j - h * H, EA + 1:EA + 2],
                                                        None, ALU.is_equal)
                            else:
                                r = rec1[:, ds(i * RING + j, 1), :]
                                ins = dve.tensor_scalar(hot[:, j, :], iota[:, :], r[:, 0, 1:2], r[:, 0, 2:3],
                                                        ALU.is_equal, ALU.mult)
                            ins.then_inc(S["hot_done"], 1)
                    for j in range(RING):
                        off = dve.value_load(blkoff[int(lastp)][0:1, ds(i * RING + j, 1)], min_val=0,
                                             max_val=(NB - 1) * P)
                        dve.wait_ge(S["agg_mm"], NT * a + CR + j + 1 + i * RING)
                        dve.wait_ge(S["acc_done"], NT * a + 2 + j + i * RING)
                        w = 4 if lastp else 2
                        tgt = accT[:, 0:w, ds(off, P)]
                        dve.tensor_tensor(tgt, tgt, bank[j % 2][:, 0:w * P].rearrange("p (w n) -> p w n", w=w),
                                          ALU.add).then_inc(S["acc_done"], 1)

            def batch_stats(d, buf, gamma, beta, l):
                base = 4 + 4 * NG * (d + 1)
                for g0, n in ((0, NG - 1), (NG - 1, 1)):
                    with dve.Fori(g0, g0 + n) as g:
                        for m in range(DH):
                            for hh in range(2):
                                dve.wait_ge(S["ev_done"], base + m * 2 + hh + 1 + g * 4)
                                w = HC if g0 == 0 else min(HC, N - (NG - 1) * GC - hh * HC)
                                dve.bn_stats(bst[:, m, ds(g * 2 + hh, 1), :],
                                             accT[:, buf + m, ds(g * GC + hh * HC, w)]).then_inc(S["bn_stat"], 1)
                dve.wait_ge(S["bn_stat"], 4 * NG * (d + 1) + 2 * d)
                for m in range(DH):
                    dve.bn_aggr(bmv[:, m, :], bst[:, m, :, :].rearrange("p a b -> p (a b)")).then_inc(S["bn_stat"], 1)
                dve.wait_ge(S["bn_sd"], d + 1)
                c(dve.reciprocal(brs[:, :], bsd[:, :]))
                lo = slice(l * DH, l * DH + DH)
                c(dve.tensor_tensor(bsc[:, :], brs[:, :], vec[gamma][:, lo], ALU.mult))
                c(dve.tensor_tensor(bms[:, :], bmv[:, :, 0], bsc[:, :], ALU.mult))
                dve.tensor_tensor(bbi[:, :], vec[beta][:, lo], bms[:, :], ALU.subtract).then_inc(S["bn_dve"], 1)

            dve.wait_ge(S["vec_in"], 16 * (len(COLS) + 4 + 6 + 1))
            rows_from_columns(0)
            for l in range(L):
                accumulate(l)
                batch_stats(2 * l, 2, "L0_gnn_g1", "L0_gnn_be1", l)
                batch_stats(2 * l + 1, 0, "L0_gnn_g_out", "L0_gnn_b_out", l)
                rows_from_columns(l + 1)
            dve.wait_ge(S["ev_T"], 4 * NG + 3 * NG * AG)
            row_stats(1)
            c(dve.tensor_scalar(eps2[:, :], epsv[:, :], 2.0, None, ALU.add))
            c(dve.memset(accT[:, 2, :], 0.0))
            c(dve.memset(accT[:, 3, :], 0.0))
            for m in range(DH):
                c(dve.tensor_scalar(accT[:, 2 + m, :], accT[:, 2 + m, :], vec["L1_gnn_ee_b1"][:, m:m + 1], 0.0,
                                    ALU.add, ALU.max))
            with dve.Fori(0, NG) as g:
                for j in range(G):
                    if j == 0:
                        dve.wait_ge(S["tab_done"], 16 * NG * (AG - 1) + 16 + g * 16)
                    dve.wait_ge(S["ln_act"], (NB + 1) + 1 + j + 1 + g * G)
                    dve.tensor_tensor(stN[:, j, :], stF[:, j * D:j * D + D],
                                      rows["L1_gnn_ee_b2"][:, :], ALU.add).then_inc(S["init_done"], 1)
                dve.wait_ge(S["init_done"], G + g * G)
                dve.sem_inc(S["stN_done"], 1)
                for m in range(DH):
                    for hh in range(2):
                        n = 3 if hh == 0 else 2
                        dve.wait_ge(S["tr_done"], 4 * NG + 3 * NG * AG + m * 2 + hh + 1 + g * 4)
                        ins = dve.tensor_scalar(accT[:, m, ds(g * GC + hh * 3 * P, n * P)],
                                                bank[4 + m * 2 + hh][:, 0:n * P], eps2[:, 0:1],
                                                vec["L1_gnn_ee_b2"][:, m:m + 1], ALU.mult, ALU.add)
                        ins.then_inc(S["ev_T"], 1)
                dve.wait_ge(S["ev_T"], 4 * NG + 3 * NG * AG + 4 + g * 4)
                dve.sem_inc(S["self_done"], 1)
            accumulate(AG - 1)
            with dve.Fori(0, NG) as g:
                for m in range(DH):
                    for hh in range(2):
                        q = m * 2 + hh
                        dve.wait_ge(S["mm_done"], 4 * NG * (2 * L + 1) + q + 1 + g * 4)
                        sl = accT[:, m, ds(g * GC + hh * HC, HC)]
                        dve.tensor_tensor(sl, sl, bank[q][:, 0:HC], ALU.add).then_inc(S["ev_done"], 1)
            with dve.Fori(0, NB) as b:
                for s, (mm, zz, n) in enumerate((("m_mm1", "m_z1", "L1_gnn_b1"), ("m_mm2", "m_z2", "L1_gnn_b2"))):
                    dve.wait_ge(S[mm], b + 1)
                    for q in range(2):
                        dve.tensor_tensor(z[s][:, q * 512:q * 512 + 512], bank[(0, 4)[s] + q][:, :],
                                          rows[n][:, q * 512:q * 512 + 512], ALU.add).then_inc(S[zz], 1)
                    dve.wait_ge(S[zz], 2 + b * 5)
                    for q in range(2):
                        dve.bn_stats(mst[s][:, q, :], z[s][:, q * 512:q * 512 + 512]).then_inc(S[zz], 1)
                    dve.wait_ge(S[zz], 4 + b * 5)
                    dve.nop(nofuse=True)
                    dve.bn_aggr(mmv[s][:, :], mst[s][:, :, :].rearrange("p a b -> p (a b)")).then_inc(S[zz], 1)
                    dve.wait_ge(S["m_sd"], s + 1 + b * 3)
                    dve.reciprocal(mrs[s][:, :], msd[s][:, :]).then_inc(S["m_rs"], 1)
                    dve.wait_ge(S["m_rs"], s + 1 + b * 3)
                    dve.scalar_tensor_tensor(mnb[s][:, :], mmv[s][:, 0:1], -1.0, mrs[s][:, :], ALU.mult, ALU.mult
                                             ).then_inc(S["m_n" + "12"[s]], 1)
                dve.wait_ge(S["m_mm3"], b + 1)
                dve.wait_ge(S["m_y"], 1 + b * 8)
                dve.tensor_tensor(y[:, :], bank[6][:, 0:D], rows["L1_gnn_b3"][:, :], ALU.add).then_inc(S["m_y"], 1)
                dve.wait_ge(S["m_h1"], 16 * NG + 16 + b * 16)
                dve.wait_ge(S["m_y"], 2 + b * 8)
                dve.tensor_tensor(y[:, :], y[:, :], h1b[:, :], ALU.add).then_inc(S["m_y"], 1)
                dve.wait_ge(S["m_y"], 3 + b * 8)
                dve.bn_stats(yst[:, :], y[:, :]).then_inc(S["m_y"], 1)
                dve.wait_ge(S["m_y"], 4 + b * 8)
                dve.nop(nofuse=True)
                dve.bn_aggr(ymv[:, :], yst[:, :]).then_inc(S["m_y"], 1)
                dve.wait_ge(S["m_sd"], 3 + b * 3)
                dve.reciprocal(yrs[:, :], ysd[:, :]).then_inc(S["m_rs"], 1)
                dve.wait_ge(S["m_rs"], 3 + b * 3)
                dve.tensor_scalar(y[:, :], y[:, :], ymv[:, 0:1], yrs[:, 0:1], ALU.subtract, ALU.mult
                                  ).then_inc(S["m_y"], 1)
                dve.wait_ge(S["m_y"], 6 + b * 8)
                dve.tensor_tensor(y[:, :], y[:, :], rows["L1_gnn_bn_g"][:, :], ALU.mult).then_inc(S["m_y"], 1)
                dve.wait_ge(S["m_y"], 7 + b * 8)
                dve.tensor_tensor(y[:, :], y[:, :], rows["L1_gnn_bn_b"][:, :], ALU.add).then_inc(S["m_y"], 1)
                dve.wait_ge(S["m_y"], 8 + b * 8)
                dve.scalar_tensor_tensor(y[:, :], y[:, :], 0.0, x_nm[:, ds(b, 1), :], ALU.max, ALU.add
                                         ).then_inc(S["m_out"], 1)
                dve.wait_ge(S["m_st"], 16 + b * 16)
                dve.sem_inc(S["m_y"], 1)

        @block.scalar
        def _(act):
            act.sem_inc(S["ev_done"], 4)
            act.sem_inc(S["aT_done"], 2)
            act.sem_inc(S["emb_done"], 2)
            act.sem_inc(S["m_o"], 3)
            act.sem_inc(S["m_y"], 1)
            for s in range(2):
                with act.Fori(0, NBP // 2) as i:
                    for r in range(2):
                        act.wait_ge(S["sort_pe_t"], NBP * s + r + 1 + i * 2)
                        act.copy(tot[:, r, :, :].rearrange("p c m -> p (c m)"), bank[4 + r][0:TC, 0:CH * EP]
                                 ).then_inc(S["sort_act_t"], 1)
            for s in range(2):
                act.wait_ge(S["pos_done"], s + 1)
                for i0, n in ((0, 1), (1, ET // SC - 1)):
                    with act.Fori(i0, i0 + n) as i:
                        for h, (a, b) in enumerate(((0, SCA), (SCA, SC))):
                            if i0 or s:
                                act.wait_ge(S["scat_" + "ab"[h]], 16 * (b - a) * (ET // SC) * s + i * (16 * (b - a)))
                            act.nop(nofuse=True)
                            cols = ds(i * SC + a, b - a)
                            act.copy(ridx[:, a:b], pos[s][:, cols]).then_inc(S["rec_act"], 1)
                            if s == 0:
                                act.copy(rr1[:, a:b, 0].bitcast(I32), dsti[:, cols]).then_inc(S["rec_act"], 1)
                                act.copy(rr1[:, a:b, 1], locf[0][:, cols]).then_inc(S["rec_act"], 1)
                                act.copy(rr1[:, a:b, 2], wgt[:, cols]).then_inc(S["rec_act"], 1)
                                act.wait_ge(S["rec_act"], 4 + h * 4 + i * 8)
                            else:
                                act.copy(rr2[:, a:b, EA + 2].bitcast(I32), srci[:, cols]).then_inc(S["rec_act"], 1)
                                act.copy(rr2[:, a:b, EA + 1], locf[1][:, cols]).then_inc(S["rec_act"], 1)
                                act.wait_ge(S["rec_act"], 8 * (ET // SC) + 3 + h * 3 + i * 6)
                                act.wait_ge(S["attr_" + "ab"[h]], 16 + i * 16)
                            act.sem_inc(S["rec1_filled"], 1)

            def ln_rows(r):
                act.wait_ge(S["ln_dve"], 2 * NB * (r + 1) + r)
                act.activation(sd[:, :], mv[:, :, 1], ACT.Sqrt, bias=epsc[:, 0:1]).then_inc(S["ln_act"], 1)
                act.wait_ge(S["ln_dve"], (2 * NB + 1) * (r + 1))
                flat = stF
                with act.Fori(0, NG) as g:
                    for j in range(G):
                        if j == 0:
                            act.wait_ge(S["stT_free"], (AG * NG + NG) * r + 1 + g)
                        act.activation(flat[:, j * D:j * D + D], x_nm[:, ds(g * G + j, 1), :], ACT.Relu,
                                       bias=nb[:, ds(g * G + j, 1)], scale=rs[:, ds(g * G + j, 1)]
                                       ).then_inc(S["ln_act"], 1)

            def evacuate(d, buf, name, l):
                with act.Fori(0, NG) as g:
                    for m in range(DH):
                        for hh in range(2):
                            q = m * 2 + hh
                            act.wait_ge(S["mm_done"], 4 * NG * d + q + 1 + g * 4)
                            act.activation(accT[:, buf + m, ds(g * GC + hh * HC, HC)], bank[q][:, 0:HC], ACT.Identity,
                                           bias=vec[name][:, l * DH + m:l * DH + m + 1]).then_inc(S["ev_done"], 1)

            def to_stage(u):
                with act.Fori(0, NG) as g:
                    act.wait_ge(S["stT_free"], NG + NG * u + 1 + g)
                    act.nop(nofuse=True)
                    for m in range(DH):
                        src = accT[:, m, ds(g * GC, GC)]
                        if u:
                            act.activation(stT[:, m, :], src, ACT.Relu, bias=bbi[:, m:m + 1], scale=bsc[:, m:m + 1]
                                           ).then_inc(S["st_done"], 1)
                        else:
                            act.copy(stT[:, m, :], src).then_inc(S["st_done"], 1)
                    act.wait_ge(S["st_done"], 2 * NG * u + 2 + g * 2)
                    if 0 < u < L:
                        act.nop(nofuse=True)
                        for m in range(DH):
                            act.copy(accT[:, m, ds(g * GC, GC)], stT[:, m, :]).then_inc(S["app_done"], 1)
                        act.wait_ge(S["app_done"], 4 * NG * u - 2 * NG + 2 + g * 2)
                    act.sem_inc(S["self_done"], 1)

            def bn_sd(d):
                act.wait_ge(S["bn_stat"], (4 * NG + 2) * (d + 1))
                act.activation(bsd[:, :], bmv[:, :, 1], ACT.Sqrt, bias=epsc[:, 0:1]).then_inc(S["bn_sd"], 1)

            act.wait_ge(S["consts"], 11)
            act.wait_ge(S["x_in"], 32)
            ln_rows(0)
            act.wait_ge(S["vec_in"], 16 * (len(COLS) + 4 + 6 + 1))
            evacuate(0, 0, "L0_gnn_b_in", 0)
            act.wait_ge(S["ev_done"], 4 + 4 * NG)
            to_stage(0)
            for l in range(L):
                evacuate(1 + 2 * l, 2, "L0_gnn_b1", l)
                bn_sd(2 * l)
                act.wait_ge(S["bn_dve"], 2 * l + 1)
                with act.Fori(0, NG) as g:
                    for m in range(DH):
                        sl = accT[:, 2 + m, ds(g * GC, GC)]
                        act.activation(sl, sl, ACT.Relu, bias=bbi[:, m:m + 1], scale=bsc[:, m:m + 1]
                                       ).then_inc(S["app_done"], 1)
                evacuate(2 + 2 * l, 0, "L0_gnn_b2", l)
                bn_sd(2 * l + 1)
                act.wait_ge(S["bn_dve"], 2 * l + 2)
                to_stage(l + 1)
            ln_rows(1)
            with act.Fori(0, NI) as i:
                for j in range(RING):
                    act.wait_ge(S["tr2_done"], j + 1 + i * RING)
                    act.wait_ge(S["r_done"], j + 1 + i * RING)
                    act.copy(aT[:, j % 2, :], bank[2 + j % 2][0:EA + 1, 0:P]).then_inc(S["aT_done"], 1)
                    act.wait_ge(S["r_done"], 2 + j + 1 + i * RING)
                    act.wait_ge(S["agg_mm"], NT * (AG - 1) + CR - 1 + j + i * RING)
                    act.activation(emb[:, j % 2, :], bank[4 + j % 2][:, 0:D], ACT.Relu).then_inc(S["emb_done"], 1)
            act.wait_ge(S["ev_done"], 4 + 4 * NG * (2 * L + 2))
            with act.Fori(0, NB) as b:
                act.wait_ge(S["m_o"], 3 + b * 3)
                act.nop(nofuse=True)
                for m in range(DH):
                    act.copy(hblk[:, m, :], accT[:, m, ds(b * P, P)]).then_inc(S["m_blk"], 1)
                for s, (zz, nn, tt, aa, gg, bb) in enumerate((("m_z1", "m_n1", "m_t1", "m_a1", "L1_gnn_g1", "L1_gnn_be1"),
                                                              ("m_z2", "m_n2", "m_t2", "m_a2", "L1_gnn_g2", "L1_gnn_be2"))):
                    act.wait_ge(S[zz], 5 + b * 5)
                    act.activation(msd[s][:, :], mmv[s][:, 1:2], ACT.Sqrt, bias=epsc[:, 0:1]).then_inc(S["m_sd"], 1)
                    act.wait_ge(S[nn], 1 + b)
                    act.activation(z[s][:, :], z[s][:, :], ACT.Identity, bias=mnb[s][:, 0:1], scale=mrs[s][:, 0:1]
                                   ).then_inc(S["m_blk"], 1)
                    for kk in range(KH):
                        act.wait_ge(S[tt], kk // 4 + 1 + b * 2)
                        act.activation(zT[s][:, kk, :], bank[(2, 2)[s] + kk // 4][:, kk % 4 * P:kk % 4 * P + P], ACT.Relu,
                                       bias=mvec[bb][:, kk:kk + 1], scale=mvec[gg][:, kk:kk + 1]).then_inc(S[aa], 1)
                act.wait_ge(S["m_y"], 5 + b * 8)
                act.activation(ysd[:, :], ymv[:, 1:2], ACT.Sqrt, bias=epsc[:, 0:1]).then_inc(S["m_sd"], 1)
                act.wait_ge(S["m_out"], 1 + b)
                act.sem_inc(S["m_o"], 3)

        @block.tensor
        def _(pe):
            pe.sem_inc(S["agg_mm"], CR)
            pe.sem_inc(S["stT_free"], 1)
            pe.sem_inc(S["r_done"], 2)
            pe.wait_ge(S["consts"], 11)
            for s in range(2):
                pe.wait_ge(S["cnt_done"], s + 1)
                pe.matmul(bank[0][0:NBP, 0:P], cnt[:, :], onesf[0:EP, :], start=True, stop=True).then_inc(S["totb_done"], 1)
                pe.wait_ge(S["pad_done"], s + 1)
                pe.matmul(bank[1][:, 0:NBP], padf[:, :], U25[:, :], start=True, stop=True)
                pe.matmul(bank[2][0:NBP, 0:1], V25[:, :], padf[:, 0:1], start=True, stop=True).then_inc(S["starts_done"], 1)
                pe.wait_ge(S["ended_done"], s + 1)
                pe.matmul(bank[3][0:1, 0:NT], onesf[0:NBP, 0:1], ended, start=True, stop=True).then_inc(S["blk_done"], 1)
                if s:
                    pe.wait_ge(S["sort_dve_r"], NBP)

                def ranks(b, r, first):
                    n = NBP * s + b
                    if not first:
                        pe.wait_ge(S["sort_act_t"], n - 1)
                        pe.wait_ge(S["sort_dve_r"], n - 1)
                    for c in range(CH):
                        ins = pe.matmul(bank[4 + r][0:TC, c * EP:(c + 1) * EP], OH[:, ds(b, 1), c * TC:(c + 1) * TC]
                                        .rearrange("p a t -> p (a t)"), onesb, start=True, stop=True)
                    ins.then_inc(S["sort_pe_t"], 1)
                    pe.matmul(bank[6 + r][0:EP, 0:ETP], Lm, OH[:, ds(b, 1), :], start=True, stop=False)
                    pe.wait_ge(S["sort_act_t"], n + 1)
                    for c in range(CH):
                        ins = pe.matmul(bank[6 + r][0:EP, 0:ETP], tot[:, r, c, :], U[:, c, :], start=False,
                                        stop=c == CH - 1)
                    ins.then_inc(S["sort_pe_r"], 1)

                ranks(0, 0, True)
                ranks(1, 1, True)
                with pe.Fori(1, NBP // 2) as i:
                    for r in range(2):
                        ranks(i * 2 + r, r, False)

            def rows_to_columns(base_tr, base_ln, base_ev, first):
                flat = stF
                with pe.Fori(0, NG) as g:
                    pe.wait_ge(S["ln_act"], base_ln + G + g * G)
                    if not first:
                        pe.wait_ge(S["ev_T"], base_ev + g * 4)
                    for m in range(DH):
                        for hh in range(2):
                            n = 3 if hh == 0 else 2
                            for j in range(n):
                                jj = hh * 3 + j
                                ins = pe.transpose(bank[4 + m * 2 + hh][:, j * P:j * P + P],
                                                   flat[:, jj * D + m * P:jj * D + m * P + P], ident[:, :])
                            ins.then_inc(S["tr_done"], 1)
                    if first:
                        pe.wait_ge(S["ev_T"], 4 + g * 4)
                    else:
                        pe.wait_ge(S["m_h1"], 16 + g * 16)
                        pe.wait_ge(S["init_done"], G + g * G)
                    pe.wait_ge(S["tr_done"], base_tr + 4 + g * 4)
                    pe.sem_inc(S["stT_free"], 1)

            def linear(d, lhs, buf, ready=None):
                with pe.Fori(0, NG) as g:
                    if ready:
                        pe.wait_ge(S[ready[0]], ready[1] + g * ready[2])
                    for m in range(DH):
                        for hh in range(2):
                            q = m * 2 + hh
                            pe.wait_ge(S["ev_done"], 4 * NG * d + q + 1 + g * 4)
                            for kk in range(DH):
                                ins = pe.matmul(bank[q][:, 0:HC], lhs[:, kk, m * P:m * P + P],
                                                accT[:, buf + kk, ds(g * GC + hh * HC, HC)], start=kk == 0,
                                                stop=kk == DH - 1)
                            ins.then_inc(S["mm_done"], 1)

            def columns_to_rows(u):
                with pe.Fori(0, NG) as g:
                    pe.wait_ge(S["st_done"], 2 * NG * u + 2 + g * 2)
                    pe.wait_ge(S["ev_T"], 4 * NG + 3 * NG * u + g * 3)
                    for q in range(3):
                        for j in range(2 * q, min(2 * q + 2, G)):
                            for m in range(DH):
                                o = (j - 2 * q) * D + m * P
                                ins = pe.transpose(bank[4 + q][:, o:o + P], stT[:, m, j * P:j * P + P], ident[:, :])
                        ins.then_inc(S["tr_done"], 1)
                    pe.wait_ge(S["tr_done"], 4 * NG + 3 * NG * u + 3 + g * 3)
                    if 0 < u < L:
                        pe.wait_ge(S["app_done"], 4 * NG * u - 2 * NG + 2 + g * 2)
                    pe.sem_inc(S["stT_free"], 1)

            def one_hot_products(a):
                last = a == AG - 1
                with pe.Fori(0, NI) as i:
                    for h in range(2):
                        if last:
                            pe.wait_ge(S["ch_" + "ab"[h]], 16 + i * 16)
                        for x in range(H + 2 * last):
                            if last and x < H:
                                j = h * H + x
                                pe.wait_ge(S["aT_done"], j + 1 + i * RING)
                                pe.transpose(bank[2 + j % 2][0:EA + 1, 0:P], chunk[:, h, x, 0:EA + 1],
                                             ident[:, :]).then_inc(S["tr2_done"], 1)
                            if last and 1 <= x <= H:
                                j = h * H + x - 1
                                pe.wait_ge(S["aT_done"], 2 + j + 1 + i * RING)
                                pe.wait_ge(S["emb_done"], j + 1 + i * RING)
                                pe.matmul(bank[4 + j % 2][:, 0:D], aT[:, j % 2, :], ee1[:, :], start=True, stop=True
                                          ).then_inc(S["r_done"], 1)
                            if x >= 2 * last:
                                j = h * H + x - 2 * last
                                if x == 2 * last:
                                    pe.wait_ge(S["g_" + "ab"[h]], 16 * H * (NI * a + 1) + i * (16 * H))
                                pe.wait_ge(S["hot_done"], NT * a + j + 1 + i * RING)
                                pe.wait_ge(S["acc_done"], NT * a + j + 1 + i * RING)
                                if last:
                                    pe.wait_ge(S["emb_done"], 2 + j + 1 + i * RING)
                                for w in range(4 if last else 2):
                                    lhs = ring[:, j, w * P:w * P + P] if w < 2 else emb[:, j % 2, (w - 2) * P:(w - 1) * P]
                                    ins = pe.matmul(bank[j % 2][:, w * P:w * P + P], lhs, hot[:, j, :], start=True,
                                                    stop=True)
                                ins.then_inc(S["agg_mm"], 1)

            pe.wait_ge(S["sort_dve_r"], 2 * NBP)
            rows_to_columns(0, 1, 0, True)
            pe.wait_ge(S["w_in"], 16 * (1 + 2 * L + 3))
            linear(0, W_in, 2)
            columns_to_rows(0)
            for l in range(L):
                one_hot_products(l)
                pe.wait_ge(S["acc_done"], NT * (l + 1) + 2)
                linear(1 + 2 * l, W1[:, l, :, :], 0)
                linear(2 + 2 * l, W2[:, l, :, :], 2, ("app_done", 4 * NG * l + 2, 2))
                columns_to_rows(l + 1)
            rows_to_columns(4 * NG + 3 * NG * AG, NB + 2, 4 * NG + 3 * NG * AG, False)
            pe.wait_ge(S["ev_T"], 8 * NG + 3 * NG * AG)
            one_hot_products(AG - 1)
            pe.wait_ge(S["acc_done"], NT * AG + 2)
            linear(2 * L + 1, ee2, 2)
            pe.wait_ge(S["wl1_in"], 48)
            with pe.Fori(0, NB) as b:
                pe.wait_ge(S["m_blk"], 2 + b * 4)
                for q in range(2):
                    for kk in range(DH):
                        ins = pe.matmul(bank[q][:, :], hblk[:, kk, :], w1[:, kk, q * 512:q * 512 + 512],
                                        start=kk == 0, stop=kk == DH - 1)
                ins.then_inc(S["m_mm1"], 1)

                def turn(s):
                    pe.wait_ge(S["m_blk"], 3 + s + b * 4)
                    for kk in range(KH):
                        ins = pe.transpose(bank[2 + kk // 4][:, kk % 4 * P:kk % 4 * P + P], z[s][:, kk * P:kk * P + P],
                                           ident[:, :])
                        if kk % 4 == 3:
                            ins.then_inc(S["m_t" + "12"[s]], 1)

                turn(0)
                for q in range(2):
                    for kk in range(KH):
                        pe.wait_ge(S["m_a1"], kk + 1 + b * KH)
                        ins = pe.matmul(bank[4 + q][:, :], zT[0][:, kk, :], w2[:, kk, q * 512:q * 512 + 512],
                                        start=kk == 0, stop=kk == KH - 1)
                ins.then_inc(S["m_mm2"], 1)
                turn(1)
                for kk in range(KH):
                    pe.wait_ge(S["m_a2"], kk + 1 + b * KH)
                    ins = pe.matmul(bank[6][:, 0:D], zT[1][:, kk, :], w3[:, kk, :], start=kk == 0, stop=kk == KH - 1)
                ins.then_inc(S["m_mm3"], 1)


_INS = ['x', 'src', 'dst', 'edge_attr_64', 'edge_weight', 'L0_gnn_W_in', 'L0_gnn_b_in', 'L0_gnn_W1', 'L0_gnn_b1',
        'L0_gnn_g1', 'L0_gnn_be1', 'L0_gnn_W2', 'L0_gnn_b2', 'L0_gnn_g_out', 'L0_gnn_b_out', 'L1_gnn_eps',
        'L1_gnn_ee_w1', 'L1_gnn_ee_b1', 'L1_gnn_ee_w2', 'L1_gnn_ee_b2', 'L1_gnn_w1', 'L1_gnn_b1', 'L1_gnn_g1',
        'L1_gnn_be1', 'L1_gnn_w2', 'L1_gnn_b2', 'L1_gnn_g2', 'L1_gnn_be2', 'L1_gnn_w3', 'L1_gnn_b3', 'L1_gnn_bn_g',
        'L1_gnn_bn_b']


def kernel(**inputs):
    import numpy as np
    import concourse.bacc as bacc
    from concourse.bass_utils import run_bass_kernel_spmd as run

    nc = bacc.Bacc("TRN2", target_bir_lowering=False, num_devices=1)
    arrays, tensors = {}, {}
    for name in _INS:
        a = np.ascontiguousarray(inputs[name])
        if a.ndim == 0:
            a = a.reshape(1)
        arrays[f"in_{name}"] = a
        tensors[name] = nc.dram_tensor(f"in_{name}", a.shape, mybir.dt.from_np(a.dtype), kind="ExternalInput").ap()
    out = nc.dram_tensor("out_0", (N, D), F32, kind="ExternalOutput").ap()
    build(nc, tensors, out)
    r = run(nc, [arrays], core_ids=[0])
    return r.results[0]["out_0"]
```

```python
from contextlib import ExitStack

import concourse.bass as bass
from concourse import mybir

F32 = mybir.dt.float32
BF16 = mybir.dt.bfloat16
I32 = mybir.dt.int32
ALU = mybir.AluOpType
ACT = mybir.ActivationFunctionType
AX = mybir.AxisListType
ds = bass.ds

P = 128
N = 3125
D = 256
DH = D // P
NB = -(-N // P)
NP = NB * P
LASTR = N - (NB - 1) * P
E = 53125
EP = 125
ET = E // EP
CH = 4
TC = -(-ET // CH)
ETP = CH * TC
NBP = NB + 1
EA = 64
REC = 68
H = 5
Q = 4
RING = Q * H
HOT = 2 * H
NT = -(-(E + NB * (P - 1)) // P)
NT = -(-NT // RING) * RING
NI = NT // RING
SC = 25
SCA = 13
STEPS = ET // SC
CUTS = (0, 4, 8, 12, STEPS)
G = 5
NG = NB // G
GC = G * P
HC = GC // 2
L = 3
HID = 1024
KH = HID // P
EPS = 1e-5
assert EP * ET == E and ET % SC == 0 and NB == G * NG


def build(nc, t, out):
    with ExitStack() as ctx:
        def sb(name, shape, dt=F32):
            return ctx.enter_context(nc.sbuf_tensor(name, shape, dt))

        def ps(name, shape, dt=F32):
            return ctx.enter_context(nc.psum_tensor(name, shape, dt))

        def sem(name):
            return ctx.enter_context(nc.semaphore(name))

        table = nc.dram_tensor("table", [NP, D], F32, kind="Internal").ap()
        h1_rows = nc.dram_tensor("h1_rows", [NP, D], F32, kind="Internal").ap()
        rec1_d = nc.dram_tensor("rec1_d", [P * NT, 4], F32, kind="Internal").ap()
        rec2_d = nc.dram_tensor("rec2_d", [P * NT, REC], F32, kind="Internal").ap()

        accT = sb("accT", [P, 4, NP])
        x_nm = sb("x_nm", [P, NB, D])
        rec1 = sb("rec1", [P, NT, 4])
        work = sb("work", [P, RING * D + HOT * P + DH * GC])
        ring = work[:, 0:RING * D].rearrange("p (j f) -> p j f", f=D)
        hot = work[:, RING * D:RING * D + HOT * P].rearrange("p (j f) -> p j f", f=P)
        stT = work[:, RING * D + HOT * P:].rearrange("p (m c) -> p m c", m=DH)
        stF = work[:, RING * D + HOT * P:]
        stR = stF.rearrange("p (b f) -> p b f", f=D)
        mlp = work[:, 0:4 * HID]
        stN = sb("stN", [P, G, D])
        W_in = sb("W_in", [P, DH, D])
        W1 = sb("W1", [P, L, DH, D])
        W2 = sb("W2", [P, L, DH, D])
        ee2 = sb("ee2", [P, DH, D])
        ee1 = sb("ee1", [EA + 1, D])
        region = sb("region", [P, HID * DH + HID * KH + D * KH])
        w1 = region[:, 0:HID * DH].rearrange("p (k n) -> p k n", k=DH)
        w2 = region[:, HID * DH:HID * (DH + KH)].rearrange("p (k n) -> p k n", k=KH)
        w3 = region[:, HID * (DH + KH):].rearrange("p (k n) -> p k n", k=KH)
        cur = [0]

        def carve(parts, cols, dt=F32):
            w = cols if dt != BF16 else -(-cols // 2)
            a = region[0:parts, cur[0]:cur[0] + w]
            cur[0] += w
            assert cur[0] <= region.shape[1]
            return a if dt == F32 else a.bitcast(dt)

        cur2 = [0]

        def carve2(parts, cols, dt=F32):
            w = cols if dt != BF16 else -(-cols // 2)
            a = ring[:, :, :].rearrange("p j f -> p (j f)")[0:parts, cur2[0]:cur2[0] + w]
            cur2[0] += w
            assert cur2[0] <= RING * D
            return a if dt == F32 else a.bitcast(dt)

        OH = carve(EP, NBP * ETP, BF16).rearrange("p (b t) -> p b t", b=NBP)
        rr2 = region[0:EP, 0:SC * REC].rearrange("p (j f) -> p j f", f=REC)
        srci = carve(EP, ETP, I32)
        dsti = carve(EP, ETP, I32)
        wgt = carve(EP, ETP)
        keyi = carve(EP, ETP, I32)
        keyf = carve(EP, ETP)
        loci = carve(EP, ETP, I32)
        locf = [carve(EP, ETP) for _ in range(2)]
        posf = carve(EP, ETP)
        term = carve(EP, ETP)
        pos = [carve(EP, ETP, I32) for _ in range(2)]
        low = carve(EP, ETP, I32)
        tot = carve2(TC, 2 * CH * EP, BF16).rearrange("p (r c m) -> p r c m", r=2, c=CH)
        U = carve2(TC, CH * ETP, BF16).rearrange("p (c t) -> p c t", c=CH)
        Lm = carve(EP, EP + 1, BF16)[:, 0:EP]
        onesb = carve(EP, EP + 1, BF16)[:, 0:EP]
        blk128 = carve2(NBP, NT)
        ended = carve2(NBP, NT)
        cnt = sb("cnt", [EP, NBP])
        padi = sb("padi", [NBP, P], I32)
        padf = sb("padf", [NBP, P])
        start = sb("start", [P, NBP])
        end = sb("end", [NBP, 1])
        U25 = sb("U25", [NBP, NBP])
        V25 = sb("V25", [NBP, NBP])
        blkoff = [sb(f"blkoff{s}", [1, NT], I32) for s in range(2)]
        fill1 = sb("fill1", [P, 44, 4])
        rr1 = sb("rr1", [EP, SC, 4])
        ridx = sb("ridx", [EP, SC], I32)
        gidx = sb("gidx", [P, RING], I32)
        chunk = sb("chunk", [P, Q, H, REC])
        fill2 = chunk[:, :, :, :].rearrange("p a j f -> p (a j) f")
        aT = sb("aT", [EA + 1, 2, P])
        emb = sb("emb", [P, 2, D])
        iota = sb("iota", [P, P])
        ident = sb("ident", [P, P])
        onesf = sb("onesf", [P, P])
        epsc = sb("epsc", [P, 1])
        st = sb("st", [P, NB, 6])
        mv = sb("mv", [P, NB, 2])
        sd = sb("sd", [P, NB])
        rs = sb("rs", [P, NB])
        nb = sb("nb", [P, NB])
        bst = sb("bst", [P, DH, 2 * NG, 6])
        bmv = sb("bmv", [P, DH, 2])
        bsd = sb("bsd", [P, DH])
        brs = sb("brs", [P, DH])
        bsc = sb("bsc", [P, DH])
        bms = sb("bms", [P, DH])
        bbi = sb("bbi", [P, DH])
        LATE = {"L1_gnn_b1": (0, HID), "L1_gnn_b3": (HID, D), "L1_gnn_bn_g": (HID + D, D)}
        COLS = [("L0_gnn_b_in", 1)] + [(f"L0_gnn_{n}", L) for n in ("b1", "g1", "be1", "b2", "g_out", "b_out")] + \
               [("L1_gnn_ee_b1", 1), ("L1_gnn_ee_b2", 1)]
        vec = {n: sb("v_" + n, [P, k * DH]) for n, k in COLS}
        mvec = {n: sb("v_" + n, [P, KH]) for n in ("L1_gnn_g1", "L1_gnn_be1", "L1_gnn_g2", "L1_gnn_be2")}
        rows = {n: sb("r_" + n, [P, k]) for n, k in (("L1_gnn_b1", HID), ("L1_gnn_b2", HID), ("L1_gnn_b3", D),
                                                     ("L1_gnn_bn_g", D), ("L1_gnn_bn_b", D), ("L1_gnn_ee_b2", D))
                if n not in LATE}
        flat1 = rec1[:, :, :].rearrange("p t f -> p (t f)")
        for n, (o, k) in LATE.items():
            rows[n] = flat1[:, o:o + k]
        epsv = sb("epsv", [P, 1])
        eps2 = sb("eps2", [P, 1])
        hblk = sb("hblk", [P, DH, P])
        z = [mlp[:, s * HID:s * HID + HID] for s in range(2)]
        zT = [mlp[:, (2 + s) * HID:(3 + s) * HID].rearrange("p (k n) -> p k n", k=KH) for s in range(2)]
        mst = [sb(f"mst{s}", [P, 2, 6]) for s in range(2)]
        mmv = [sb(f"mmv{s}", [P, 2]) for s in range(2)]
        msd = [sb(f"msd{s}", [P, 1]) for s in range(2)]
        mrs = [sb(f"mrs{s}", [P, 1]) for s in range(2)]
        mnb = [sb(f"mnb{s}", [P, 1]) for s in range(2)]
        h1b = stN[:, 0, :]
        y = stN[:, 1, :]
        yst = sb("yst", [P, 6])
        ymv = sb("ymv", [P, 2])
        ysd = sb("ysd", [P, 1])
        yrs = sb("yrs", [P, 1])
        ynb = sb("ynb", [P, 1])

        bank = [ps(f"bank{i}", [P, 512]) for i in range(8)]

        names = """keys_done edges_in x_in fills filled1 filled2 w_in vec_in scat_a scat_b rec1_in
            stN_done tab_done ln_act m_h1 agg_mm m_y m_hb m_out m_st consts rec1_filled
            pos_done rec2_copied idx_done dve_c acc_done cnt_done totb_done pad_done
            starts_done ended_done blk_done sort_pe_r sort_dve_r ln_dve tr_done ev_T self_done
            hot_done ev_done bn_stat bn_sd bn_dve init_done mm_done m_mm1 m_mm2 m_z1 m_z2 m_sd1
            m_sd2 m_rs1 m_rs2 m_n1 m_n2 m_mm3 m_sdy late_in aT_done emb_done sort_pe_t
            sort_act_t rec_act stT_free st_done app_done wl1_in tr2_done r_done m_blk m_nz1
            m_nz2 m_t1 m_t2 m_a1 m_a2 attr_a attr_b g0 g1 g2 g3 ch0 ch1 ch2 ch3""".split()
        S = {n: sem(n) for n in names}
        block = ctx.enter_context(nc.Block())
        AG = 4
        CR = RING
        AC = H
        YC = 9

        def dram_T(ap, k):
            return ap.rearrange("(k p) n -> p k n", p=P)

        def skewed(eng, parts):
            lead, lag = max(k for k, _ in parts), -min(k for k, _ in parts)

            def step(i):
                for shift, part in parts:
                    if not isinstance(i, int) or 0 <= i + shift < NB:
                        part(i + shift)

            for i in range(-lead, lag):
                step(i)
            with eng.Fori(lag, NB - lead) as i:
                step(i)
            for i in range(NB - lead, NB + lag):
                step(i)

        @block.sync
        def _(sp):
            v = lambda n: t[n].rearrange("(p t) -> p t", p=EP)
            sp.wait_ge(S["keys_done"], 1)
            sp.dma_start(srci[:, 0:ET], v("src")).then_inc(S["edges_in"], 16)
            sp.dma_start(dsti[:, 0:ET], v("dst")).then_inc(S["edges_in"], 16)
            sp.dma_start(wgt[:, 0:ET], v("edge_weight")).then_inc(S["edges_in"], 16)
            sp.dma_start(x_nm[:, 0:NB - 1, :], t["x"][0:(NB - 1) * P, :].rearrange("(b p) f -> p b f", p=P)
                         ).then_inc(S["x_in"], 16)
            sp.dma_start(x_nm[0:LASTR, NB - 1, :], t["x"][(NB - 1) * P:N, :]).then_inc(S["x_in"], 16)
            sp.wait_ge(S["fills"], 1)
            for q in range(NT // 44):
                sp.dma_start(rec1_d.rearrange("(p t) f -> p t f", p=P)[:, q * 44:(q + 1) * 44, :], fill1[:, :, :]
                             ).then_inc(S["filled1"], 16)
            for q in range(NT // RING):
                sp.dma_start(rec2_d.rearrange("(p t) f -> p t f", p=P)[:, q * RING:(q + 1) * RING, :],
                             fill2[:, :, :]).then_inc(S["filled2"], 16)
            sp.dma_start(W_in[:, :, :], dram_T(t["L0_gnn_W_in"], DH)).then_inc(S["w_in"], 16)
            for l in range(L):
                sp.dma_start(W1[:, l, :, :], dram_T(t["L0_gnn_W1"][l], DH)).then_inc(S["w_in"], 16)
                sp.dma_start(W2[:, l, :, :], dram_T(t["L0_gnn_W2"][l], DH)).then_inc(S["w_in"], 16)
            sp.dma_start(ee2[:, :, :], dram_T(t["L1_gnn_ee_w2"], DH)).then_inc(S["w_in"], 16)
            sp.dma_start(ee1[0:EA, :], t["L1_gnn_ee_w1"]).then_inc(S["w_in"], 16)
            sp.dma_start(ee1[EA:EA + 1, :], t["L1_gnn_ee_b1"].rearrange("(a n) -> a n", a=1)).then_inc(S["w_in"], 16)
            for n, k in COLS:
                a = t[n] if k == 1 else t[n].rearrange("l f -> (l f)")
                sp.dma_start(vec[n][:, :], a.rearrange("(c p) -> p c", p=P), allow_slow_non_contiguous=True).then_inc(S["vec_in"], 16)
            for n in mvec:
                sp.dma_start(mvec[n][:, :], t[n].rearrange("(c p) -> p c", p=P), allow_slow_non_contiguous=True).then_inc(S["vec_in"], 16)
            for n in rows:
                if n in LATE:
                    continue
                sp.dma_start(rows[n][:, :], t[n].partition_broadcast(P)
                             ).then_inc(S["vec_in"], 16)
            sp.dma_start(epsv[:, :], t["L1_gnn_eps"].partition_broadcast(P)).then_inc(S["vec_in"], 16)
            av = t["edge_attr_64"].rearrange("(p t) f -> p t f", p=EP)

            def attributes(a):
                with sp.Fori(CUTS[a], CUTS[a + 1]) as i:
                    for h, (lo, hi) in enumerate(((0, SCA), (SCA, SC))):
                        sp.wait_ge(S["scat_" + "ab"[h]], 16 * (hi - lo) * STEPS + i * (16 * (hi - lo)))
                        sp.dma_start(rr2[:, lo:hi, 0:EA], av[:, ds(i * SC + lo, hi - lo), :]
                                     ).then_inc(S["attr_" + "ab"[h]], 16)

            sp.wait_ge(S["scat_a"], 16 * SCA * STEPS)
            sp.wait_ge(S["scat_b"], 16 * (SC - SCA) * STEPS)
            sp.dma_start(rec1[:, :, :], rec1_d.rearrange("(p t) f -> p t f", p=P)).then_inc(S["rec1_in"], 16)
            sp.wait_ge(S["fills"], 2)
            tv = table.rearrange("(b p) f -> p b f", p=P)
            hv = h1_rows.rearrange("(b p) f -> p b f", p=P)
            for u in range(AG - 1):
                with sp.Fori(0, NG) as g:
                    sp.wait_ge(S["stN_done"], NG * u + 1 + g)
                    sp.dma_start(tv[:, ds(g * G, G), :], stN[:, :, :]).then_inc(S["tab_done"], 16)
                attributes(u)
            attributes(AG - 1)
            with sp.Fori(0, NG) as g:
                sp.wait_ge(S["ln_act"], NB + 2 + G + g * G)
                sp.dma_start(hv[:, ds(g * G, G), :], stR).then_inc(S["m_h1"], 16)
                sp.wait_ge(S["stN_done"], NG * (AG - 1) + 1 + g)
                sp.dma_start(tv[:, ds(g * G, G), :], stN[:, :, :]).then_inc(S["tab_done"], 16)
            rv = rec2_d.rearrange("(p t) f -> p t f", p=P)
            sp.wait_ge(S["scat_a"], 2 * 16 * SCA * STEPS)
            sp.wait_ge(S["scat_b"], 2 * 16 * (SC - SCA) * STEPS)
            with sp.Fori(0, NI) as i:
                for q in range(Q):
                    sp.wait_ge(S["agg_mm"], NT * (AG - 1) + H * q + H + i * RING)
                    sp.dma_start(chunk[:, q, :, :], rv[:, ds(i * RING + q * H, H), :]).then_inc(S[f"ch{q}"], 16)
            sp.wait_ge(S["m_h1"], 16 * NG)

            def mlp_rows(b, last):
                sp.wait_ge(S["m_y"], YC - 6 + b * 8)
                sp.wait_ge(S["m_hb"], 1)
                sp.dma_start(h1b, h1_rows[ds(b * P, P), :]).then_inc(S["m_h1"], 16)
                sp.wait_ge(S["m_out"], b + 1)
                if last:
                    sp.dma_start(out[b * P:N, :], y[0:LASTR, :]).then_inc(S["m_st"], 16)
                else:
                    sp.dma_start(out[ds(b * P, P), :], y).then_inc(S["m_st"], 16)

            with sp.Fori(0, NB - 1) as b:
                mlp_rows(b, False)
            mlp_rows(NB - 1, True)
            sp.wait_ge(S["m_st"], 16 + 16 * NB)

        @block.gpsimd
        def _(pool):
            k = [0]

            def c(ins):
                k[0] += 1
                ins.then_inc(S["consts"], 1)
                pool.wait_ge(S["consts"], k[0])

            c(pool.iota(iota[:, :], [[1, P]], base=0, channel_multiplier=0, allow_small_or_imprecise_dtypes=True))
            c(pool.iota(blk128, [[P, NT]], base=0, channel_multiplier=0, allow_small_or_imprecise_dtypes=True))
            c(pool.memset(onesf[:, :], 1.0))
            c(pool.memset(onesb, 1.0))
            c(pool.memset(epsc[:, :], EPS))
            c(pool.affine_select(out=ident[:, :], in_=onesf[:, :], compare_op=ALU.is_equal, fill=0.0, base=0,
                                 pattern=[[1, P]], channel_multiplier=-1))
            c(pool.affine_select(out=Lm, in_=onesb, compare_op=ALU.is_gt, fill=0.0, base=0,
                                 pattern=[[1, EP]], channel_multiplier=-1))
            c(pool.memset(U, 1.0))
            c(pool.affine_select(out=U, in_=U, compare_op=ALU.is_gt, fill=0.0, base=0,
                                 pattern=[[-TC, CH], [1, ETP]], channel_multiplier=-1))
            c(pool.affine_select(out=U25[:, :], in_=onesf[0:NBP, 0:NBP], compare_op=ALU.is_gt, fill=0.0, base=0,
                                 pattern=[[1, NBP]], channel_multiplier=-1))
            c(pool.affine_select(out=V25[:, :], in_=onesf[0:NBP, 0:NBP], compare_op=ALU.is_ge, fill=0.0, base=0,
                                 pattern=[[1, NBP]], channel_multiplier=-1))
            halves = ((0, SCA), (SCA, SC))

            def scatter(rec, rd, h):
                for j in range(*halves[h]):
                    pool.indirect_dma_start(rd[:, :], bass.IndirectOffsetOnAxis(ap=ridx[:, j:j + 1], axis=0),
                                            rec[:, j, :], None).then_inc(S["scat_" + "ab"[h]], 16)

            pool.wait_ge(S["filled1"], 16 * (NT // 44))
            with pool.Fori(0, STEPS) as i:
                for h in range(2):
                    pool.wait_ge(S["rec1_filled"], 1 + h + i * 2)
                    pool.nop(nofuse=True)
                    scatter(rr1, rec1_d, h)
            pool.wait_ge(S["rec1_in"], 16)
            pool.wait_ge(S["filled2"], 16 * (NT // RING))
            pool.wait_ge(S["pos_done"], 2)

            def second_scatter(a):
                with pool.Fori(CUTS[a], CUTS[a + 1]) as i:
                    for h, (lo, hi) in enumerate(halves):
                        pool.wait_ge(S["scat_" + "ab"[h]], 16 * (hi - lo) * STEPS + i * (16 * (hi - lo)))
                        pool.wait_ge(S["attr_" + "ab"[h]], 16 + i * 16)
                        pool.nop(nofuse=True)
                        cols = ds(i * SC + lo, hi - lo)
                        pool.tensor_copy(ridx[:, lo:hi], pos[1][:, cols]).then_inc(S["rec2_copied"], 1)
                        pool.tensor_copy(rr2[:, lo:hi, EA + 2].bitcast(I32), srci[:, cols]).then_inc(S["rec2_copied"], 1)
                        pool.tensor_copy(rr2[:, lo:hi, EA + 1], locf[1][:, cols]).then_inc(S["rec2_copied"], 1)
                        pool.wait_ge(S["rec2_copied"], 3 + h * 3 + i * 6)
                        pool.nop(nofuse=True)
                        scatter(rr2, rec2_d, h)

            for a in range(AG):
                pool.wait_ge(S["tab_done"], 16 * NG * (a + 1) + 16)
                with pool.Fori(0, NI) as i:
                    for q in range(Q):
                        pool.wait_ge(S["agg_mm"], NT * a + H * q + H + i * RING)
                        if a < AG - 1:
                            idx = rec1[:, ds(i * RING + q * H, H), 0]
                        else:
                            pool.wait_ge(S[f"ch{q}"], 16 + i * 16)
                            idx = chunk[:, q, :, EA + 2]
                        pool.nop(nofuse=True)
                        pool.tensor_copy(gidx[:, q * H:q * H + H], idx.bitcast(I32)).then_inc(S["idx_done"], 1)
                        pool.wait_ge(S["idx_done"], NI * Q * a + q + 1 + i * Q)
                        pool.nop(nofuse=True)
                        for j in range(q * H, q * H + H):
                            pool.indirect_dma_start(ring[:, j, :], None, table[:, :],
                                                    bass.IndirectOffsetOnAxis(ap=gidx[:, j:j + 1], axis=0)
                                                    ).then_inc(S[f"g{q}"], 16)
                if a < AG - 1:
                    second_scatter(a)
                if a == AG - 2:
                    second_scatter(AG - 1)

        @block.vector
        def _(dve):
            k = [0]

            def c(ins):
                k[0] += 1
                ins.then_inc(S["dve_c"], 1)
                dve.wait_ge(S["dve_c"], k[0])

            dve.sem_inc(S["acc_done"], AC)
            dve.sem_inc(S["m_y"], YC)
            dve.sem_inc(S["m_st"], 16)
            dve.sem_inc(S["tab_done"], 16)
            c(dve.memset(x_nm[:, NB - 1, :], 0.0))
            c(dve.memset(srci, 0))
            c(dve.memset(dsti, 0))
            dve.memset(wgt, 0.0).then_inc(S["keys_done"], 1)
            c(dve.memset(fill1[:, :, :], 0.0))
            c(dve.memset(fill1[:, :, 1], -1.0))
            c(dve.memset(fill2[:, :, :], 0.0))
            dve.memset(fill2[:, :, EA + 1], -1.0).then_inc(S["fills"], 1)
            dve.wait_ge(S["fills"], 1)
            c(dve.memset(rr1[:, :, 3], 0.0))
            dve.wait_ge(S["edges_in"], 48)
            dve.wait_ge(S["consts"], 11)
            for s, arr in enumerate((srci, dsti)):
                c(dve.tensor_scalar(keyi, arr, 7, None, ALU.arith_shift_right))
                c(dve.tensor_copy(keyf, keyi))
                c(dve.memset(keyf[:, ET:ETP], -1.0))
                c(dve.tensor_scalar(loci, arr, P - 1, None, ALU.bitwise_and))
                c(dve.tensor_copy(locf[s], loci))
                for b in range(NBP):
                    c(dve.tensor_scalar(OH[:, b, :], keyf, float(b), None, ALU.is_equal))
                dve.tensor_reduce(cnt[:, :], OH, AX.X, ALU.add).then_inc(S["cnt_done"], 1)
                dve.wait_ge(S["totb_done"], s + 1)
                c(dve.tensor_copy(padi[:, :], bank[0][0:NBP, 0:P]))
                c(dve.tensor_scalar(padi[:, :], padi[:, :], P - 1, None, ALU.add))
                c(dve.tensor_scalar(padi[:, :], padi[:, :], 7, None, ALU.arith_shift_right))
                dve.tensor_scalar(padf[:, :], padi[:, :], float(P), None, ALU.mult).then_inc(S["pad_done"], 1)
                dve.wait_ge(S["starts_done"], s + 1)
                c(dve.tensor_copy(start[:, :], bank[1][:, 0:NBP]))
                c(dve.tensor_copy(end[:, :], bank[2][0:NBP, 0:1]))
                dve.tensor_scalar(ended, blk128, end[:, 0:1], None, ALU.is_ge).then_inc(S["ended_done"], 1)
                dve.wait_ge(S["blk_done"], s + 1)
                c(dve.tensor_scalar(blkoff[s][:, :], bank[3][0:1, 0:NT], float(NB - 1), float(P), ALU.min, ALU.mult))
                c(dve.memset(posf, 0.0))
                for b in range(NBP):
                    dve.wait_ge(S["sort_pe_r"], NBP * s + b + 1)
                    dve.scalar_tensor_tensor(term, bank[6 + b % 2][0:EP, 0:ETP], start[0:EP, b:b + 1], OH[:, b, :],
                                             ALU.add, ALU.mult).then_inc(S["sort_dve_r"], 1)
                    dve.wait_ge(S["sort_dve_r"], NBP * s + b + 1)
                    c(dve.tensor_tensor(posf, posf, term, ALU.add))
                c(dve.tensor_copy(keyi, posf))
                c(dve.tensor_scalar(low, keyi, P - 1, None, ALU.bitwise_and))
                c(dve.tensor_scalar(keyi, keyi, 7, None, ALU.arith_shift_right))
                dve.scalar_tensor_tensor(pos[s], low, float(NT), keyi, ALU.mult, ALU.add).then_inc(S["pos_done"], 1)
                dve.wait_ge(S["pos_done"], s + 1)
            c(dve.memset(rr2[:, :, EA + 3], 0.0))
            dve.memset(rr2[:, :, EA], 1.0).then_inc(S["fills"], 1)

            def row_stats(r):
                with dve.Fori(0, NG) as g:
                    for j in range(G):
                        dve.bn_stats(st[:, ds(g * G + j, 1), :], x_nm[:, ds(g * G + j, 1), :]).then_inc(S["ln_dve"], 1)
                dve.wait_ge(S["ln_dve"], (2 * r + 1) * NB + r)
                for b in range(NB):
                    dve.bn_aggr(mv[:, b, :], st[:, b, :]).then_inc(S["ln_dve"], 1)
                dve.wait_ge(S["ln_act"], r * (NB + 1) + 1)
                c(dve.reciprocal(rs[:, :], sd[:, :]))
                dve.scalar_tensor_tensor(nb[:, :], mv[:, :, 0], -1.0, rs[:, :], ALU.mult, ALU.mult
                                         ).then_inc(S["ln_dve"], 1)

            dve.wait_ge(S["x_in"], 32)
            row_stats(0)
            pT = [bank[4], bank[5]]
            with dve.Fori(0, NG) as g:
                for m in range(DH):
                    for hh in range(2):
                        n = 3 if hh == 0 else 2
                        dve.wait_ge(S["tr_done"], m * 2 + hh + 1 + g * 4)
                        dve.tensor_copy(accT[:, 2 + m, ds(g * GC + hh * 3 * P, n * P)], bank[4 + m * 2 + hh][:, 0:n * P]
                                        ).then_inc(S["ev_T"], 1)

            def rows_from_columns(u):
                with dve.Fori(0, NG) as g:
                    for q in range(3):
                        n = 2 if q < 2 else 1
                        dve.wait_ge(S["tr_done"], 4 * NG + u * 3 * NG + q + 1 + g * 3)
                        src = bank[4 + q][:, 0:n * D].rearrange("p (b f) -> p b f", f=D)
                        if u < AG - 1:
                            if q == 0:
                                dve.wait_ge(S["tab_done"], 16 * NG * u + 16 + g * 16)
                            ins = dve.tensor_copy(stN[:, 2 * q:2 * q + n, :], src)
                            ins.then_inc(S["ev_T"], 1)
                            if q == 2:
                                dve.wait_ge(S["ev_T"], 4 * NG + u * 3 * NG + 3 + g * 3)
                                dve.sem_inc(S["stN_done"], 1)
                        else:
                            xs = x_nm[:, ds(g * G + 2 * q, n), :]
                            dve.tensor_tensor(xs, xs, src, ALU.add).then_inc(S["ev_T"], 1)

            def accumulate(a):
                dve.wait_ge(S["self_done"], NG * (a + 1 + (a == AG - 1)))
                if a == 0:
                    dve.wait_ge(S["rec1_in"], 16)
                lastp = a == AG - 1
                banks = 2 if lastp else H
                w = 4 if lastp else 2
                with dve.Fori(0, NI) as i:
                    for q in range(Q):
                        dve.wait_ge(S["agg_mm"], NT * a + (q + 1) * H - HOT + CR + i * RING)
                        if lastp:
                            dve.wait_ge(S[f"ch{q}"], 16 + i * 16)
                        for j in range(q * H, q * H + H):
                            if lastp:
                                ins = dve.tensor_scalar(hot[:, j % HOT, :], iota[:, :],
                                                        chunk[:, q, j - q * H, EA + 1:EA + 2], None, ALU.is_equal)
                            else:
                                r = rec1[:, ds(i * RING + j, 1), :]
                                ins = dve.tensor_scalar(hot[:, j % HOT, :], iota[:, :], r[:, 0, 1:2], r[:, 0, 2:3],
                                                        ALU.is_equal, ALU.mult)
                            ins.then_inc(S["hot_done"], 1)
                        for j in range(q * H, q * H + H):
                            off = dve.value_load(blkoff[int(lastp)][0:1, ds(i * RING + j, 1)], min_val=0,
                                                 max_val=(NB - 1) * P)
                            dve.wait_ge(S["agg_mm"], NT * a + CR + j + 1 + i * RING)
                            dve.wait_ge(S["acc_done"], NT * a + AC + j + i * RING)
                            tgt = accT[:, 0:w, ds(off, P)]
                            dve.tensor_tensor(tgt, tgt, bank[j % banks][:, 0:w * P].rearrange("p (w n) -> p w n", w=w),
                                              ALU.add).then_inc(S["acc_done"], 1)

            def batch_stats(d, buf, gamma, beta, l):
                base = 4 + 4 * NG * (d + 1)
                for g0, n in ((0, NG - 1), (NG - 1, 1)):
                    with dve.Fori(g0, g0 + n) as g:
                        for m in range(DH):
                            for hh in range(2):
                                dve.wait_ge(S["ev_done"], base + m * 2 + hh + 1 + g * 4)
                                w = HC if g0 == 0 else min(HC, N - (NG - 1) * GC - hh * HC)
                                dve.bn_stats(bst[:, m, ds(g * 2 + hh, 1), :],
                                             accT[:, buf + m, ds(g * GC + hh * HC, w)]).then_inc(S["bn_stat"], 1)
                dve.wait_ge(S["bn_stat"], 4 * NG * (d + 1) + 2 * d)
                for m in range(DH):
                    dve.bn_aggr(bmv[:, m, :], bst[:, m, :, :].rearrange("p a b -> p (a b)")).then_inc(S["bn_stat"], 1)
                dve.wait_ge(S["bn_sd"], d + 1)
                c(dve.reciprocal(brs[:, :], bsd[:, :]))
                lo = slice(l * DH, l * DH + DH)
                c(dve.tensor_tensor(bsc[:, :], brs[:, :], vec[gamma][:, lo], ALU.mult))
                c(dve.tensor_tensor(bms[:, :], bmv[:, :, 0], bsc[:, :], ALU.mult))
                dve.tensor_tensor(bbi[:, :], vec[beta][:, lo], bms[:, :], ALU.subtract).then_inc(S["bn_dve"], 1)

            dve.wait_ge(S["vec_in"], 16 * (len(COLS) + 4 + len(rows) - len(LATE) + 1))
            rows_from_columns(0)
            for l in range(L):
                accumulate(l)
                batch_stats(2 * l, 2, "L0_gnn_g1", "L0_gnn_be1", l)
                batch_stats(2 * l + 1, 0, "L0_gnn_g_out", "L0_gnn_b_out", l)
                rows_from_columns(l + 1)
            dve.wait_ge(S["ev_T"], 4 * NG + 3 * NG * AG)
            row_stats(1)
            c(dve.tensor_scalar(eps2[:, :], epsv[:, :], 2.0, None, ALU.add))
            c(dve.memset(accT[:, 2, :], 0.0))
            c(dve.memset(accT[:, 3, :], 0.0))
            for m in range(DH):
                c(dve.tensor_scalar(accT[:, 2 + m, :], accT[:, 2 + m, :], vec["L1_gnn_ee_b1"][:, m:m + 1], 0.0,
                                    ALU.add, ALU.max))
            with dve.Fori(0, NG) as g:
                for j in range(G):
                    if j == 0:
                        dve.wait_ge(S["tab_done"], 16 * NG * (AG - 1) + 16 + g * 16)
                    dve.wait_ge(S["ln_act"], (NB + 1) + 1 + j + 1 + g * G)
                    dve.tensor_tensor(stN[:, j, :], stF[:, j * D:j * D + D],
                                      rows["L1_gnn_ee_b2"][:, :], ALU.add).then_inc(S["init_done"], 1)
                dve.wait_ge(S["init_done"], G + g * G)
                dve.sem_inc(S["stN_done"], 1)
                for m in range(DH):
                    for hh in range(2):
                        n = 3 if hh == 0 else 2
                        dve.wait_ge(S["tr_done"], 4 * NG + 3 * NG * AG + m * 2 + hh + 1 + g * 4)
                        ins = dve.tensor_scalar(accT[:, m, ds(g * GC + hh * 3 * P, n * P)],
                                                bank[4 + m * 2 + hh][:, 0:n * P], eps2[:, 0:1],
                                                vec["L1_gnn_ee_b2"][:, m:m + 1], ALU.mult, ALU.add)
                        ins.then_inc(S["ev_T"], 1)
                dve.wait_ge(S["ev_T"], 4 * NG + 3 * NG * AG + 4 + g * 4)
                dve.sem_inc(S["self_done"], 1)
            accumulate(AG - 1)
            with dve.Fori(0, NG) as g:
                for m in range(DH):
                    for hh in range(2):
                        q = m * 2 + hh
                        dve.wait_ge(S["mm_done"], 4 * NG * (2 * L + 1) + q + 1 + g * 4)
                        sl = accT[:, m, ds(g * GC + hh * HC, HC)]
                        dve.tensor_tensor(sl, sl, bank[q][:, 0:HC], ALU.add).then_inc(S["ev_done"], 1)
            def mlp_norm(s, b):
                mm, zz = ("m_mm1", "m_mm2")[s], ("m_z1", "m_z2")[s]
                dve.wait_ge(S[mm], 1 + b)
                for q in range(2):
                    dve.tensor_tensor(z[s][:, q * 512:q * 512 + 512], bank[(0, 4)[s] + q][:, :],
                                      rows[("L1_gnn_b1", "L1_gnn_b2")[s]][:, q * 512:q * 512 + 512], ALU.add
                                      ).then_inc(S[zz], 1)
                dve.wait_ge(S[zz], 2 + b * 5)
                for q in range(2):
                    dve.bn_stats(mst[s][:, q, :], z[s][:, q * 512:q * 512 + 512]).then_inc(S[zz], 1)
                dve.wait_ge(S[zz], 4 + b * 5)
                dve.nop(nofuse=True)
                dve.bn_aggr(mmv[s][:, :], mst[s][:, :, :].rearrange("p a b -> p (a b)")).then_inc(S[zz], 1)
                dve.wait_ge(S[("m_sd1", "m_sd2")[s]], 1 + b)
                dve.reciprocal(mrs[s][:, :], msd[s][:, :]).then_inc(S[("m_rs1", "m_rs2")[s]], 1)
                dve.wait_ge(S[("m_rs1", "m_rs2")[s]], 1 + b)
                dve.scalar_tensor_tensor(mnb[s][:, :], mmv[s][:, 0:1], -1.0, mrs[s][:, :], ALU.mult, ALU.mult
                                         ).then_inc(S[("m_n1", "m_n2")[s]], 1)

            def mlp_result(b):
                dve.wait_ge(S["m_mm3"], 1 + b)
                dve.wait_ge(S["m_st"], 16 + b * 16)
                dve.tensor_tensor(y, bank[6][:, 0:D], rows["L1_gnn_b3"], ALU.add).then_inc(S["m_y"], 1)
                dve.wait_ge(S["m_h1"], 16 * NG + 16 + b * 16)
                dve.wait_ge(S["m_y"], YC + 1 + b * 8)
                dve.tensor_tensor(y, y, h1b, ALU.add).then_inc(S["m_y"], 1)
                dve.wait_ge(S["m_y"], YC + 2 + b * 8)
                dve.bn_stats(yst[:, :], y).then_inc(S["m_y"], 1)
                dve.wait_ge(S["m_y"], YC + 3 + b * 8)
                dve.nop(nofuse=True)
                dve.bn_aggr(ymv[:, :], yst[:, :]).then_inc(S["m_y"], 1)
                dve.wait_ge(S["m_sdy"], 1 + b)
                dve.reciprocal(yrs[:, :], ysd[:, :]).then_inc(S["m_y"], 1)
                dve.wait_ge(S["m_y"], YC + 5 + b * 8)
                dve.tensor_scalar(y, y, ymv[:, 0:1], yrs[:, 0:1], ALU.subtract, ALU.mult).then_inc(S["m_y"], 1)
                dve.wait_ge(S["m_y"], YC + 6 + b * 8)
                dve.tensor_tensor(y, y, rows["L1_gnn_bn_g"], ALU.mult).then_inc(S["m_y"], 1)
                dve.wait_ge(S["m_y"], YC + 7 + b * 8)
                dve.tensor_tensor(y, y, rows["L1_gnn_bn_b"][:, :], ALU.add).then_inc(S["m_y"], 1)
                dve.wait_ge(S["m_y"], YC + 8 + b * 8)
                dve.scalar_tensor_tensor(y, y, 0.0, x_nm[:, ds(b, 1), :].rearrange("p a f -> p (a f)"), ALU.max,
                                         ALU.add).then_inc(S["m_out"], 1)

            dve.wait_ge(S["ev_done"], 4 + 4 * NG * (2 * L + 2))
            dve.sem_inc(S["m_hb"], 1)
            dve.wait_ge(S["late_in"], 16 * len(LATE))
            skewed(dve, ((1, lambda b: mlp_norm(0, b)), (-2, mlp_result), (0, lambda b: mlp_norm(1, b))))

        @block.scalar
        def _(act):
            act.sem_inc(S["ev_done"], 4)
            act.sem_inc(S["aT_done"], 2)
            act.sem_inc(S["emb_done"], 2)
            for s in range(2):
                with act.Fori(0, NBP // 2) as i:
                    for r in range(2):
                        act.wait_ge(S["sort_pe_t"], NBP * s + r + 1 + i * 2)
                        act.copy(tot[:, r, :, :].rearrange("p c m -> p (c m)"), bank[4 + r][0:TC, 0:CH * EP]
                                 ).then_inc(S["sort_act_t"], 1)
            act.wait_ge(S["pos_done"], 1)
            for i0, n in ((0, 1), (1, STEPS - 1)):
                with act.Fori(i0, i0 + n) as i:
                    for h, (a, b) in enumerate(((0, SCA), (SCA, SC))):
                        if i0:
                            act.wait_ge(S["scat_" + "ab"[h]], i * (16 * (b - a)))
                        act.nop(nofuse=True)
                        cols = ds(i * SC + a, b - a)
                        act.copy(ridx[:, a:b], pos[0][:, cols]).then_inc(S["rec_act"], 1)
                        act.copy(rr1[:, a:b, 0].bitcast(I32), dsti[:, cols]).then_inc(S["rec_act"], 1)
                        act.copy(rr1[:, a:b, 1], locf[0][:, cols]).then_inc(S["rec_act"], 1)
                        act.copy(rr1[:, a:b, 2], wgt[:, cols]).then_inc(S["rec_act"], 1)
                        act.wait_ge(S["rec_act"], 4 + h * 4 + i * 8)
                        act.sem_inc(S["rec1_filled"], 1)

            def ln_rows(r):
                act.wait_ge(S["ln_dve"], 2 * NB * (r + 1) + r)
                act.activation(sd[:, :], mv[:, :, 1], ACT.Sqrt, bias=epsc[:, 0:1]).then_inc(S["ln_act"], 1)
                act.wait_ge(S["ln_dve"], (2 * NB + 1) * (r + 1))
                flat = stF
                with act.Fori(0, NG) as g:
                    for j in range(G):
                        if j == 0:
                            act.wait_ge(S["stT_free"], (AG * NG + NG) * r + 1 + g)
                        act.activation(flat[:, j * D:j * D + D], x_nm[:, ds(g * G + j, 1), :], ACT.Relu,
                                       bias=nb[:, ds(g * G + j, 1)], scale=rs[:, ds(g * G + j, 1)]
                                       ).then_inc(S["ln_act"], 1)

            def evacuate(d, buf, name, l):
                with act.Fori(0, NG) as g:
                    for m in range(DH):
                        for hh in range(2):
                            q = m * 2 + hh
                            act.wait_ge(S["mm_done"], 4 * NG * d + q + 1 + g * 4)
                            act.activation(accT[:, buf + m, ds(g * GC + hh * HC, HC)], bank[q][:, 0:HC], ACT.Identity,
                                           bias=vec[name][:, l * DH + m:l * DH + m + 1]).then_inc(S["ev_done"], 1)

            def to_stage(u):
                with act.Fori(0, NG) as g:
                    act.wait_ge(S["stT_free"], NG + NG * u + 1 + g)
                    act.nop(nofuse=True)
                    for m in range(DH):
                        src = accT[:, m, ds(g * GC, GC)]
                        if u:
                            act.activation(stT[:, m, :], src, ACT.Relu, bias=bbi[:, m:m + 1], scale=bsc[:, m:m + 1]
                                           ).then_inc(S["st_done"], 1)
                        else:
                            act.copy(stT[:, m, :], src).then_inc(S["st_done"], 1)
                    act.wait_ge(S["st_done"], 2 * NG * u + 2 + g * 2)
                    if 0 < u < L:
                        act.nop(nofuse=True)
                        for m in range(DH):
                            act.copy(accT[:, m, ds(g * GC, GC)], stT[:, m, :]).then_inc(S["app_done"], 1)
                        act.wait_ge(S["app_done"], 4 * NG * u - 2 * NG + 2 + g * 2)
                    act.sem_inc(S["self_done"], 1)

            def bn_sd(d):
                act.wait_ge(S["bn_stat"], (4 * NG + 2) * (d + 1))
                act.activation(bsd[:, :], bmv[:, :, 1], ACT.Sqrt, bias=epsc[:, 0:1]).then_inc(S["bn_sd"], 1)

            act.wait_ge(S["consts"], 11)
            act.wait_ge(S["x_in"], 32)
            ln_rows(0)
            act.wait_ge(S["vec_in"], 16 * (len(COLS) + 4 + len(rows) - len(LATE) + 1))
            evacuate(0, 0, "L0_gnn_b_in", 0)
            act.wait_ge(S["ev_done"], 4 + 4 * NG)
            to_stage(0)
            for l in range(L):
                evacuate(1 + 2 * l, 2, "L0_gnn_b1", l)
                bn_sd(2 * l)
                act.wait_ge(S["bn_dve"], 2 * l + 1)
                with act.Fori(0, NG) as g:
                    for m in range(DH):
                        sl = accT[:, 2 + m, ds(g * GC, GC)]
                        act.activation(sl, sl, ACT.Relu, bias=bbi[:, m:m + 1], scale=bsc[:, m:m + 1]
                                       ).then_inc(S["app_done"], 1)
                evacuate(2 + 2 * l, 0, "L0_gnn_b2", l)
                bn_sd(2 * l + 1)
                act.wait_ge(S["bn_dve"], 2 * l + 2)
                to_stage(l + 1)
            ln_rows(1)
            act.wait_ge(S["scat_a"], 2 * 16 * SCA * STEPS)
            act.wait_ge(S["scat_b"], 2 * 16 * (SC - SCA) * STEPS)
            act.wait_ge(S["acc_done"], AC + NT * (AG - 1))
            act.dma_start(w1, dram_T(t["L1_gnn_w1"], DH)).then_inc(S["wl1_in"], 16)
            act.dma_start(w2, dram_T(t["L1_gnn_w2"], KH)).then_inc(S["wl1_in"], 16)
            act.dma_start(w3, dram_T(t["L1_gnn_w3"], KH)).then_inc(S["wl1_in"], 16)
            for n in LATE:
                act.dma_start(rows[n], t[n].partition_broadcast(P)).then_inc(S["late_in"], 16)
            with act.Fori(0, NI) as i:
                for j in range(RING):
                    act.wait_ge(S["tr2_done"], j + 1 + i * RING)
                    act.wait_ge(S["r_done"], j + 1 + i * RING)
                    act.copy(aT[:, j % 2, :], bank[2 + j % 2][0:EA + 1, 0:P]).then_inc(S["aT_done"], 1)
                    act.wait_ge(S["r_done"], 2 + j + 1 + i * RING)
                    act.wait_ge(S["agg_mm"], NT * (AG - 1) + CR - 1 + j + i * RING)
                    act.activation(emb[:, j % 2, :], bank[4 + j % 2][:, 0:D], ACT.Relu).then_inc(S["emb_done"], 1)

            def block_columns(b):
                if not isinstance(b, int) or b:
                    act.wait_ge(S["m_mm1"], b)
                act.nop(nofuse=True)
                for m in range(DH):
                    act.copy(hblk[:, m, :], accT[:, m, ds(b * P, P)]).then_inc(S["m_blk"], 1)

            def normalise(s, b):
                act.wait_ge(S[("m_z1", "m_z2")[s]], 5 + b * 5)
                act.activation(msd[s][:, :], mmv[s][:, 1:2], ACT.Sqrt, bias=epsc[:, 0:1]
                               ).then_inc(S[("m_sd1", "m_sd2")[s]], 1)
                act.wait_ge(S[("m_n1", "m_n2")[s]], 1 + b)
                act.activation(z[s], z[s], ACT.Identity, bias=mnb[s][:, 0:1], scale=mrs[s][:, 0:1]
                               ).then_inc(S[("m_nz1", "m_nz2")[s]], 1)

            def turned(s, b):
                for kk in range(KH):
                    act.wait_ge(S[("m_t1", "m_t2")[s]], kk // 4 + 1 + b * 2)
                    act.activation(zT[s][:, kk, :], bank[2 + kk // 4][:, kk % 4 * P:kk % 4 * P + P], ACT.Relu,
                                   bias=mvec[("L1_gnn_be1", "L1_gnn_be2")[s]][:, kk:kk + 1],
                                   scale=mvec[("L1_gnn_g1", "L1_gnn_g2")[s]][:, kk:kk + 1]
                                   ).then_inc(S[("m_a1", "m_a2")[s]], 1)

            def result_deviation(b):
                act.wait_ge(S["m_y"], YC + 4 + b * 8)
                act.activation(ysd[:, :], ymv[:, 1:2], ACT.Sqrt, bias=epsc[:, 0:1]).then_inc(S["m_sdy"], 1)

            act.wait_ge(S["ev_done"], 4 + 4 * NG * (2 * L + 2))
            skewed(act, ((1, lambda b: normalise(0, b)), (2, block_columns), (-1, lambda b: turned(1, b)),
                         (-2, result_deviation), (1, lambda b: turned(0, b)), (0, lambda b: normalise(1, b))))

        @block.tensor
        def _(pe):
            pe.sem_inc(S["agg_mm"], CR)
            pe.sem_inc(S["stT_free"], 1)
            pe.sem_inc(S["r_done"], 2)
            pe.wait_ge(S["consts"], 11)
            for s in range(2):
                pe.wait_ge(S["cnt_done"], s + 1)
                pe.matmul(bank[0][0:NBP, 0:P], cnt[:, :], onesf[0:EP, :], start=True, stop=True).then_inc(S["totb_done"], 1)
                pe.wait_ge(S["pad_done"], s + 1)
                pe.matmul(bank[1][:, 0:NBP], padf[:, :], U25[:, :], start=True, stop=True)
                pe.matmul(bank[2][0:NBP, 0:1], V25[:, :], padf[:, 0:1], start=True, stop=True).then_inc(S["starts_done"], 1)
                pe.wait_ge(S["ended_done"], s + 1)
                pe.matmul(bank[3][0:1, 0:NT], onesf[0:NBP, 0:1], ended, start=True, stop=True).then_inc(S["blk_done"], 1)
                if s:
                    pe.wait_ge(S["sort_dve_r"], NBP)

                def ranks(b, r, first):
                    n = NBP * s + b
                    if not first:
                        pe.wait_ge(S["sort_act_t"], n - 1)
                        pe.wait_ge(S["sort_dve_r"], n - 1)
                    for c in range(CH):
                        ins = pe.matmul(bank[4 + r][0:TC, c * EP:(c + 1) * EP], OH[:, ds(b, 1), c * TC:(c + 1) * TC]
                                        .rearrange("p a t -> p (a t)"), onesb, start=True, stop=True)
                    ins.then_inc(S["sort_pe_t"], 1)
                    pe.matmul(bank[6 + r][0:EP, 0:ETP], Lm, OH[:, ds(b, 1), :], start=True, stop=False)
                    pe.wait_ge(S["sort_act_t"], n + 1)
                    for c in range(CH):
                        ins = pe.matmul(bank[6 + r][0:EP, 0:ETP], tot[:, r, c, :], U[:, c, :], start=False,
                                        stop=c == CH - 1)
                    ins.then_inc(S["sort_pe_r"], 1)

                ranks(0, 0, True)
                ranks(1, 1, True)
                with pe.Fori(1, NBP // 2) as i:
                    for r in range(2):
                        ranks(i * 2 + r, r, False)

            def rows_to_columns(base_tr, base_ln, base_ev, first):
                flat = stF
                with pe.Fori(0, NG) as g:
                    pe.wait_ge(S["ln_act"], base_ln + G + g * G)
                    if not first:
                        pe.wait_ge(S["ev_T"], base_ev + g * 4)
                    for m in range(DH):
                        for hh in range(2):
                            n = 3 if hh == 0 else 2
                            for j in range(n):
                                jj = hh * 3 + j
                                ins = pe.transpose(bank[4 + m * 2 + hh][:, j * P:j * P + P],
                                                   flat[:, jj * D + m * P:jj * D + m * P + P], ident[:, :])
                            ins.then_inc(S["tr_done"], 1)
                    if first:
                        pe.wait_ge(S["ev_T"], 4 + g * 4)
                    else:
                        pe.wait_ge(S["m_h1"], 16 + g * 16)
                        pe.wait_ge(S["init_done"], G + g * G)
                    pe.wait_ge(S["tr_done"], base_tr + 4 + g * 4)
                    pe.sem_inc(S["stT_free"], 1)

            def linear(d, lhs, buf, ready=None):
                with pe.Fori(0, NG) as g:
                    if ready:
                        pe.wait_ge(S[ready[0]], ready[1] + g * ready[2])
                    for m in range(DH):
                        for hh in range(2):
                            q = m * 2 + hh
                            pe.wait_ge(S["ev_done"], 4 * NG * d + q + 1 + g * 4)
                            for kk in range(DH):
                                ins = pe.matmul(bank[q][:, 0:HC], lhs[:, kk, m * P:m * P + P],
                                                accT[:, buf + kk, ds(g * GC + hh * HC, HC)], start=kk == 0,
                                                stop=kk == DH - 1)
                            ins.then_inc(S["mm_done"], 1)

            def columns_to_rows(u):
                with pe.Fori(0, NG) as g:
                    pe.wait_ge(S["st_done"], 2 * NG * u + 2 + g * 2)
                    pe.wait_ge(S["ev_T"], 4 * NG + 3 * NG * u + g * 3)
                    for q in range(3):
                        for j in range(2 * q, min(2 * q + 2, G)):
                            for m in range(DH):
                                o = (j - 2 * q) * D + m * P
                                ins = pe.transpose(bank[4 + q][:, o:o + P], stT[:, m, j * P:j * P + P], ident[:, :])
                        ins.then_inc(S["tr_done"], 1)
                    pe.wait_ge(S["tr_done"], 4 * NG + 3 * NG * u + 3 + g * 3)
                    if 0 < u < L:
                        pe.wait_ge(S["app_done"], 4 * NG * u - 2 * NG + 2 + g * 2)
                    pe.sem_inc(S["stT_free"], 1)

            def one_hot_products(a):
                last = a == AG - 1
                banks = 2 if last else H
                lag = 2 if last else 0
                with pe.Fori(0, NI) as i:
                    for q in range(Q):
                        if last:
                            pe.wait_ge(S[f"ch{q}"], 16 + i * 16)
                        for x in range(H + lag):
                            if last and x < H:
                                j = q * H + x
                                pe.wait_ge(S["aT_done"], j + 1 + i * RING)
                                pe.transpose(bank[2 + j % 2][0:EA + 1, 0:P], chunk[:, q, x, 0:EA + 1],
                                             ident[:, :]).then_inc(S["tr2_done"], 1)
                            if last and 1 <= x <= H:
                                j = q * H + x - 1
                                pe.wait_ge(S["aT_done"], 2 + j + 1 + i * RING)
                                pe.wait_ge(S["emb_done"], j + 1 + i * RING)
                                pe.matmul(bank[4 + j % 2][:, 0:D], aT[:, j % 2, :], ee1[:, :], start=True, stop=True
                                          ).then_inc(S["r_done"], 1)
                            if x >= lag:
                                j = q * H + x - lag
                                if x == lag:
                                    pe.wait_ge(S[f"g{q}"], 16 * H * (NI * a + 1) + i * (16 * H))
                                pe.wait_ge(S["hot_done"], NT * a + j + 1 + i * RING)
                                pe.wait_ge(S["acc_done"], NT * a + j - banks + 1 + AC + i * RING)
                                if last:
                                    pe.wait_ge(S["emb_done"], 2 + j + 1 + i * RING)
                                for w in range(4 if last else 2):
                                    lhs = ring[:, j, w * P:w * P + P] if w < 2 else emb[:, j % 2, (w - 2) * P:(w - 1) * P]
                                    ins = pe.matmul(bank[j % banks][:, w * P:w * P + P], lhs, hot[:, j % HOT, :],
                                                    start=True, stop=True)
                                ins.then_inc(S["agg_mm"], 1)

            pe.wait_ge(S["sort_dve_r"], 2 * NBP)
            rows_to_columns(0, 1, 0, True)
            pe.wait_ge(S["w_in"], 16 * (1 + 2 * L + 3))
            linear(0, W_in, 2)
            columns_to_rows(0)
            for l in range(L):
                one_hot_products(l)
                pe.wait_ge(S["acc_done"], NT * (l + 1) + AC)
                linear(1 + 2 * l, W1[:, l, :, :], 0)
                linear(2 + 2 * l, W2[:, l, :, :], 2, ("app_done", 4 * NG * l + 2, 2))
                columns_to_rows(l + 1)
            rows_to_columns(4 * NG + 3 * NG * AG, NB + 2, 4 * NG + 3 * NG * AG, False)
            pe.wait_ge(S["ev_T"], 8 * NG + 3 * NG * AG)
            one_hot_products(AG - 1)
            pe.wait_ge(S["acc_done"], NT * AG + AC)
            linear(2 * L + 1, ee2, 2)
            pe.wait_ge(S["wl1_in"], 48)

            def first_map(b):
                pe.wait_ge(S["m_blk"], 2 + b * 2)
                for q in range(2):
                    for kk in range(DH):
                        ins = pe.matmul(bank[q][:, :], hblk[:, kk, :], w1[:, kk, q * 512:q * 512 + 512],
                                        start=kk == 0, stop=kk == DH - 1)
                ins.then_inc(S["m_mm1"], 1)

            def turn(s, b):
                pe.wait_ge(S[("m_nz1", "m_nz2")[s]], 1 + b)
                if s == 0 and (not isinstance(b, int) or b >= 2):
                    pe.wait_ge(S["m_a2"], b * KH - KH)
                if s == 1 and (not isinstance(b, int) or b < NB - 1):
                    pe.wait_ge(S["m_a1"], b * KH + 2 * KH)
                for kk in range(KH):
                    ins = pe.transpose(bank[2 + kk // 4][:, kk % 4 * P:kk % 4 * P + P], z[s][:, kk * P:kk * P + P],
                                       ident[:, :])
                    if kk % 4 == 3:
                        ins.then_inc(S[("m_t1", "m_t2")[s]], 1)

            def second_map(b):
                for q in range(2):
                    for kk in range(KH):
                        pe.wait_ge(S["m_a1"], kk + 1 + b * KH)
                        ins = pe.matmul(bank[4 + q][:, :], zT[0][:, kk, :], w2[:, kk, q * 512:q * 512 + 512],
                                        start=kk == 0, stop=kk == KH - 1)
                ins.then_inc(S["m_mm2"], 1)

            def third_map(b):
                pe.wait_ge(S["m_y"], YC - 7 + b * 8)
                for kk in range(KH):
                    pe.wait_ge(S["m_a2"], kk + 1 + b * KH)
                    ins = pe.matmul(bank[6][:, 0:D], zT[1][:, kk, :], w3[:, kk, :], start=kk == 0, stop=kk == KH - 1)
                ins.then_inc(S["m_mm3"], 1)

            skewed(pe, ((1, first_map), (-2, third_map), (-1, lambda b: turn(1, b)), (0, second_map),
                        (1, lambda b: turn(0, b))))


_INS = ['x', 'src', 'dst', 'edge_attr_64', 'edge_weight', 'L0_gnn_W_in', 'L0_gnn_b_in', 'L0_gnn_W1', 'L0_gnn_b1',
        'L0_gnn_g1', 'L0_gnn_be1', 'L0_gnn_W2', 'L0_gnn_b2', 'L0_gnn_g_out', 'L0_gnn_b_out', 'L1_gnn_eps',
        'L1_gnn_ee_w1', 'L1_gnn_ee_b1', 'L1_gnn_ee_w2', 'L1_gnn_ee_b2', 'L1_gnn_w1', 'L1_gnn_b1', 'L1_gnn_g1',
        'L1_gnn_be1', 'L1_gnn_w2', 'L1_gnn_b2', 'L1_gnn_g2', 'L1_gnn_be2', 'L1_gnn_w3', 'L1_gnn_b3', 'L1_gnn_bn_g',
        'L1_gnn_bn_b']


def kernel(**inputs):
    import numpy as np
    import concourse.bacc as bacc
    from concourse.bass_utils import run_bass_kernel_spmd as run

    nc = bacc.Bacc("TRN2", target_bir_lowering=False, num_devices=1)
    arrays, tensors = {}, {}
    for name in _INS:
        a = np.ascontiguousarray(inputs[name])
        if a.ndim == 0:
            a = a.reshape(1)
        arrays[f"in_{name}"] = a
        tensors[name] = nc.dram_tensor(f"in_{name}", a.shape, mybir.dt.from_np(a.dtype), kind="ExternalInput").ap()
    out = nc.dram_tensor("out_0", (N, D), F32, kind="ExternalOutput").ap()
    build(nc, tensors, out)
    r = run(nc, [arrays], core_ids=[0])
    return r.results[0]["out_0"]
```

```python
from contextlib import ExitStack

import concourse.bass as bass
from concourse import mybir

F32 = mybir.dt.float32
BF16 = mybir.dt.bfloat16
I32 = mybir.dt.int32
ALU = mybir.AluOpType
ACT = mybir.ActivationFunctionType
AX = mybir.AxisListType
ds = bass.ds

P = 128
N = 3125
D = 256
DH = D // P
NB = -(-N // P)
NP = NB * P
LASTR = N - (NB - 1) * P
E = 53125
EP = 125
ET = E // EP
CH = 4
TC = -(-ET // CH)
ETP = CH * TC
NBP = NB + 1
KA = 18
EA = 64
KC = 4
KR = -(-(-(-E // P)) // KC)
KT = KC * KR
assert (KT - 1) * P < E <= KT * P
WIN = NP - P
H = 5
EB = 4
Q = 4
RING = Q * H
HOT = 2 * H
NT = -(-(E + NB * (P - 1)) // P)
NT = -(-NT // RING) * RING
NI = NT // RING
assert KT <= NT - RING
SC = 17
SCA = 9
STEPS = ET // SC
G = 5
NG = NB // G
GC = G * P
HC = GC // 2
L = 3
HID = 1024
KH = HID // P
EPS = 1e-5
assert EP * ET == E and ET % SC == 0 and NB == G * NG


def build(nc, t, out):
    with ExitStack() as ctx:
        def sb(name, shape, dt=F32):
            return ctx.enter_context(nc.sbuf_tensor(name, shape, dt))

        def ps(name, shape, dt=F32):
            return ctx.enter_context(nc.psum_tensor(name, shape, dt))

        def sem(name):
            return ctx.enter_context(nc.semaphore(name))

        table = nc.dram_tensor("table", [NP, D], F32, kind="Internal").ap()
        h1_rows = nc.dram_tensor("h1_rows", [NP, D], F32, kind="Internal").ap()
        rec1_d = nc.dram_tensor("rec1_d", [P * NT, 4], F32, kind="Internal").ap()
        rec2_d = nc.dram_tensor("rec2_d", [P * NT, EA], F32, kind="Internal").ap()
        rec3_d = nc.dram_tensor("rec3_d", [P * NT, 4], F32, kind="Internal").ap()
        e2_d = nc.dram_tensor("e2_d", [P, DH * NP], F32, kind="Internal").ap()

        accT = sb("accT", [P, 4, NP])
        x_nm = sb("x_nm", [P, NB, D])
        rec1 = sb("rec1", [P, NT, 4])
        work = sb("work", [P, RING * D + HOT * P + DH * GC])
        ring = work[:, 0:RING * D].rearrange("p (j f) -> p j f", f=D)
        hot = work[:, RING * D:RING * D + HOT * P].rearrange("p (j f) -> p j f", f=P)
        stF = work[:, RING * D + HOT * P:]
        stR = stF.rearrange("p (b f) -> p b f", f=D)
        assert NB * D <= RING * D + HOT * P
        all_rows = work[:, 0:NB * D]
        all_cols = all_rows.rearrange("p (m n) -> p m n", m=DH)
        mlp = work[:, 0:4 * HID]
        stN = sb("stN", [P, G, D])
        W_in = sb("W_in", [P, DH, D])
        W1 = sb("W1", [P, L, DH, D])
        W2 = sb("W2", [P, L, DH, D])
        ee2 = sb("ee2", [P, DH, D])
        ee1 = sb("ee1", [EA + 1, D])
        region = sb("region", [P, HID * DH + HID * KH + D * KH])
        w1 = region[:, 0:HID * DH].rearrange("p (k n) -> p k n", k=DH)
        w2 = region[:, HID * DH:HID * (DH + KH)].rearrange("p (k n) -> p k n", k=KH)
        w3 = region[:, HID * (DH + KH):].rearrange("p (k n) -> p k n", k=KH)
        cur = [0]

        def carve(parts, cols, dt=F32):
            w = cols if dt != BF16 else -(-cols // 2)
            a = region[0:parts, cur[0]:cur[0] + w]
            cur[0] += w
            assert cur[0] <= region.shape[1]
            return a if dt == F32 else a.bitcast(dt)

        cur2 = [0]

        def carve2(parts, cols, dt=F32):
            w = cols if dt != BF16 else -(-cols // 2)
            a = ring[:, :, :].rearrange("p j f -> p (j f)")[0:parts, cur2[0]:cur2[0] + w]
            cur2[0] += w
            assert cur2[0] <= RING * D
            return a if dt == F32 else a.bitcast(dt)

        OH = carve(EP, NBP * ETP, BF16).rearrange("p (b t) -> p b t", b=NBP)
        rr2 = region[0:EP, 0:SC * EA].rearrange("p (j f) -> p j f", f=EA)
        dstF = region[0:KR, 0:KC * P].rearrange("p (c e) -> p c e", e=P)
        srcF = region[0:KR, KC * P:2 * KC * P].rearrange("p (c e) -> p c e", e=P)
        srci = carve(EP, ETP, I32)
        dsti = carve(EP, ETP, I32)
        wgt = carve(EP, ETP)
        nxt = carve(EP, ETP, I32)
        dstR = carve(KR, KC * P, I32).rearrange("p (c e) -> p c e", e=P)
        srcR = carve(KR, KC * P, I32).rearrange("p (c e) -> p c e", e=P)
        meta = [carve(EP, ETP * 4).rearrange("p (t f) -> p t f", f=4) for _ in range(2)]
        keyi = carve2(EP, ETP, I32)
        keyf = carve2(EP, ETP)
        posf = carve2(EP, ETP)
        term = [carve2(EP, ETP) for _ in range(2)]
        low = carve2(EP, ETP, I32)
        tot = carve2(TC, 2 * CH * EP, BF16).rearrange("p (r c m) -> p r c m", r=2, c=CH)
        U = carve2(TC, CH * ETP, BF16).rearrange("p (c t) -> p c t", c=CH)
        Lm = carve(EP, EP + 1, BF16)[:, 0:EP]
        onesb = carve(EP, EP + 1, BF16)[:, 0:EP]
        blk128 = carve2(NBP, NT)
        ended = carve2(NBP, NT)
        junk = carve(EP, ETP, BF16)
        cnt = sb("cnt", [EP, NBP])
        padi = sb("padi", [NBP, P], I32)
        padf = sb("padf", [NBP, P])
        start = sb("start", [P, NBP])
        end = sb("end", [NBP, 1])
        U25 = sb("U25", [NBP, NBP])
        V25 = sb("V25", [NBP, NBP])
        blkoff = [sb(f"blkoff{s}", [1, NT], I32) for s in range(2)]
        fill1 = sb("fill1", [P, 44, 4])
        rr1 = sb("rr1", [EP, SC, 4])
        gidx = sb("gidx", [P, RING], I32)
        chunk = sb("chunk", [P, Q, H, EA + 1])
        fill2 = chunk[:, :, :, 0:EA].rearrange("p a j f -> p (a j) f")
        rec2 = sb("rec2", [P, NT, 2])
        first = sb("first", [KR, KC])
        bad = sb("bad", [P, KC + 1])
        general = sb("general", [1, 1], I32)
        aT = sb("aT", [EA + 1, 2, P])
        emb = sb("emb", [P, EB, D])
        iota = sb("iota", [P, P])
        ident = sb("ident", [P, P])
        onesf = sb("onesf", [P, P])
        epsc = sb("epsc", [P, 1])
        st = sb("st", [P, NB, 6])
        mv = sb("mv", [P, NB, 2])
        sd = sb("sd", [P, NB])
        rs = sb("rs", [P, NB])
        nb = sb("nb", [P, NB])
        bst = sb("bst", [P, DH, 2 * NG, 6])
        bmv = sb("bmv", [P, DH, 2])
        bsd = sb("bsd", [P, DH])
        brs = sb("brs", [P, DH])
        bsc = sb("bsc", [P, DH])
        bms = sb("bms", [P, DH])
        bbi = sb("bbi", [P, DH])
        flat1 = rec1[:, :, :].rearrange("p t f -> p (t f)")
        flat2 = chunk[:, :, :, :].rearrange("p a j f -> p (a j f)")
        LATE = {"L1_gnn_b1": (flat1, 0, HID), "L1_gnn_b3": (flat1, HID, D), "L1_gnn_bn_g": (flat1, HID + D, D),
                "L1_gnn_b2": (flat2, 0, HID), "L1_gnn_bn_b": (flat2, HID, D)}
        COLS = [("L0_gnn_b_in", 1)] + [(f"L0_gnn_{n}", L) for n in ("b1", "g1", "be1", "b2", "g_out", "b_out")] + \
               [("L1_gnn_ee_b1", 1), ("L1_gnn_ee_b2", 1)]
        vec = {n: sb("v_" + n, [P, k * DH]) for n, k in COLS}
        mvec = {n: sb("v_" + n, [P, KH]) for n in ("L1_gnn_g1", "L1_gnn_be1", "L1_gnn_g2", "L1_gnn_be2")}
        rows = {n: sb("r_" + n, [P, k]) for n, k in (("L1_gnn_b1", HID), ("L1_gnn_b2", HID), ("L1_gnn_b3", D),
                                                     ("L1_gnn_bn_g", D), ("L1_gnn_bn_b", D), ("L1_gnn_ee_b2", D))
                if n not in LATE}
        for n, (flat, o, k) in LATE.items():
            rows[n] = flat[:, o:o + k]
        epsv = sb("epsv", [P, 1])
        eps2 = sb("eps2", [P, 1])
        hblk = emb[:, 0, :].rearrange("p (m n) -> p m n", m=DH)
        z = [mlp[:, s * HID:s * HID + HID] for s in range(2)]
        zT = [mlp[:, (2 + s) * HID:(3 + s) * HID].rearrange("p (k n) -> p k n", k=KH) for s in range(2)]
        mst = [sb(f"mst{s}", [P, 2, 6]) for s in range(2)]
        mmv = [sb(f"mmv{s}", [P, 2]) for s in range(2)]
        msd = [sb(f"msd{s}", [P, 1]) for s in range(2)]
        mrs = [sb(f"mrs{s}", [P, 1]) for s in range(2)]
        mnb = [sb(f"mnb{s}", [P, 1]) for s in range(2)]
        h1b = stN[:, 0, :]
        y = stN[:, 1, :]
        yst = sb("yst", [P, 6])
        ymv = sb("ymv", [P, 2])
        ysd = sb("ysd", [P, 1])
        yrs = sb("yrs", [P, 1])
        ynb = sb("ynb", [P, 1])

        bank = [ps(f"bank{i}", [P, 512]) for i in range(8)]

        names = """rows_in rows_done rows_turned flag_done rec2_in e2_out e2_in dve_g e_hot e_mm e_acc gscat_a
            gscat_b keys_done edges_in x_in fills filled1 filled2 w_in vec_in scat_a scat_b rec1_in stN_done
            tab_done tab_odd ln_act m_h1 agg_mm m_y agg_summed e_summed m_out m_st consts rec1_copied
            hots_done cnt_rest pos_sum pos_done rec2_copied idx_done dve_c acc_done cnt_done totb_done
            pad_done starts_done ended_done blk_done sort_pe_r sort_dve_r ln_dve tr_done ev_T self_done
            hot_done ev_done bn_stat bn_sd bn_dve init_done mm_done m_mm1 m_mm2 m_z1 m_z2 m_sd1 m_sd2 m_rs1
            m_rs2 m_n1 m_n2 m_mm3 m_sdy late_in aT_done emb_done sort_pe_t sort_act_t stT_free st_done
            app_done wl1_in tr2_done r_done m_blk m_nz1 m_nz2 m_t1 m_t2 m_a1 m_a2 attr_a attr_b g0 g1 g2 g3
            ch0 ch1 ch2 ch3""".split()
        S = {n: sem(n) for n in names}
        block = ctx.enter_context(nc.Block())
        AG = 4
        CR = RING
        AC = H
        YC = 9

        def first_linear_of(l):
            return 1 + 2 * l + (l > 0)

        def rows_stored(odd, u):
            return 16 + 16 * u * (NG // 2 if odd else NG - NG // 2)

        SUMS = 3

        def dram_T(ap, k):
            return ap.rearrange("(k p) n -> p k n", p=P)

        def tiles_in_order(eng, body):
            with eng.Fori(0, NI - 2) as i:
                body(i, False)
            flag = eng.value_load(general[0:1, 0:1], min_val=0, max_val=1)
            with eng.If(flag):
                with eng.Fori(NI - 2, NI - 1) as i:
                    body(i, False)
                body(NI - 1, True)
            with eng.Else():
                body(NI - 2, True)

        def skewed(eng, parts):
            lead, lag = max(k for k, _ in parts), -min(k for k, _ in parts)

            def step(i):
                for shift, part in parts:
                    if not isinstance(i, int) or 0 <= i + shift < NB:
                        part(i + shift)

            for i in range(-lead, lag):
                step(i)
            with eng.Fori(lag, NB - lead) as i:
                step(i)
            for i in range(NB - lead, NB + lag):
                step(i)

        @block.sync
        def _(sp):
            v = lambda n: t[n].rearrange("(p t) -> p t", p=EP)
            sp.wait_ge(S["keys_done"], 1)
            sp.dma_start(srci[:, 0:ET], v("src")).then_inc(S["edges_in"], 16)
            sp.dma_start(dsti[:, 0:ET], v("dst")).then_inc(S["edges_in"], 16)
            sp.dma_start(wgt[:, 0:ET], v("edge_weight")).then_inc(S["edges_in"], 16)
            sp.dma_start(x_nm[:, 0:NB - 1, :], t["x"][0:(NB - 1) * P, :].rearrange("(b p) f -> p b f", p=P)
                         ).then_inc(S["x_in"], 16)
            sp.dma_start(x_nm[0:LASTR, NB - 1, :], t["x"][(NB - 1) * P:N, :]).then_inc(S["x_in"], 16)
            sp.dma_start(nxt[0:EP - 1, 0:ET], t["dst"][1:1 + (EP - 1) * ET].rearrange("(p t) -> p t", t=ET)
                         ).then_inc(S["rows_in"], 16)
            sp.dma_start(nxt[EP - 1:EP, 0:ET - 1], t["dst"][(EP - 1) * ET + 1:E].rearrange("(a t) -> a t", a=1)
                         ).then_inc(S["rows_in"], 16)
            for n, dest in (("dst", dstR), ("src", srcR)):
                for c in range(KC):
                    full = KR if c < KC - 1 else KR - 1
                    sp.dma_start(dest[0:full, c, :], t[n][c * KR * P:(c * KR + full) * P].rearrange("(k e) -> k e", e=P)
                                 ).then_inc(S["rows_in"], 16)
                sp.dma_start(dest[KR - 1:KR, KC - 1, 0:E - (KT - 1) * P],
                             t[n][(KT - 1) * P:E].rearrange("(a e) -> a e", a=1)).then_inc(S["rows_in"], 16)
            sp.wait_ge(S["fills"], 1)
            fill = lambda d, q: sp.dma_start(d.rearrange("(p t) f -> p t f", p=P)[:, q * 44:(q + 1) * 44, :],
                                             fill1[:, :, :])
            for q in range(NT // 44):
                fill(rec1_d, q).then_inc(S["filled1"], 16)
            sp.dma_start(W_in[:, :, :], dram_T(t["L0_gnn_W_in"], DH)).then_inc(S["w_in"], 16)
            for l in range(L):
                sp.dma_start(W1[:, l, :, :], dram_T(t["L0_gnn_W1"][l], DH)).then_inc(S["w_in"], 16)
                sp.dma_start(W2[:, l, :, :], dram_T(t["L0_gnn_W2"][l], DH)).then_inc(S["w_in"], 16)
            sp.dma_start(ee2[:, :, :], dram_T(t["L1_gnn_ee_w2"], DH)).then_inc(S["w_in"], 16)
            sp.dma_start(ee1[0:EA, :], t["L1_gnn_ee_w1"]).then_inc(S["w_in"], 16)
            sp.dma_start(ee1[EA:EA + 1, :], t["L1_gnn_ee_b1"].rearrange("(a n) -> a n", a=1)).then_inc(S["w_in"], 16)
            for n, k in COLS:
                a = t[n] if k == 1 else t[n].rearrange("l f -> (l f)")
                sp.dma_start(vec[n][:, :], a.rearrange("(c p) -> p c", p=P), allow_slow_non_contiguous=True).then_inc(S["vec_in"], 16)
            for n in mvec:
                sp.dma_start(mvec[n][:, :], t[n].rearrange("(c p) -> p c", p=P), allow_slow_non_contiguous=True).then_inc(S["vec_in"], 16)
            for n in rows:
                if n in LATE:
                    continue
                sp.dma_start(rows[n][:, :], t[n].partition_broadcast(P)
                             ).then_inc(S["vec_in"], 16)
            sp.dma_start(epsv[:, :], t["L1_gnn_eps"].partition_broadcast(P)).then_inc(S["vec_in"], 16)
            tv = table.rearrange("(b p) f -> p b f", p=P)
            hv = h1_rows.rearrange("(b p) f -> p b f", p=P)

            def store_rows(u):
                for g in range(NG):
                    sp.wait_ge(S["stN_done"], NG * u + 1 + g)
                    sp.dma_start(tv[:, g * G:(g + 1) * G, :], (stN[:, :, :], stR)[g % 2]
                                 ).then_inc(S[("tab_done", "tab_odd")[g % 2]], 16)

            store_rows(0)
            sp.wait_ge(S["flag_done"], 1)
            flag = sp.value_load(general[0:1, 0:1], min_val=0, max_val=1)
            with sp.If(flag):
                for q in range(NT // 44):
                    fill(rec3_d, q).then_inc(S["filled2"], 16)
                for q in range(NI):
                    sp.dma_start(rec2_d.rearrange("(p t) f -> p t f", p=P)[:, q * RING:(q + 1) * RING, :], fill2
                                 ).then_inc(S["filled2"], 16)
                sp.wait_ge(S["pos_done"], 2)
                av = t["edge_attr_64"].rearrange("(p t) f -> p t f", p=EP)
                for i0, n in ((0, 1), (1, STEPS - 1)):
                    with sp.Fori(i0, i0 + n) as i:
                        for h, (lo, hi) in enumerate(((0, SCA), (SCA, SC))):
                            if i0:
                                sp.wait_ge(S["gscat_" + "ab"[h]], i * (32 * (hi - lo)))
                            sp.dma_start(rr2[:, lo:hi, :], av[:, ds(i * SC + lo, hi - lo), :]
                                         ).then_inc(S["attr_" + "ab"[h]], 16)
                sp.wait_ge(S["gscat_a"], 32 * SCA * STEPS)
                sp.wait_ge(S["gscat_b"], 32 * (SC - SCA) * STEPS)
                sp.dma_start(rec2[:, :, :], rec3_d.rearrange("(p t) f -> p t f", p=P)[:, :, 0:2]
                             ).then_inc(S["rec2_in"], 16)
                rv = rec2_d.rearrange("(p t) f -> p t f", p=P)
                with sp.Fori(0, NI) as i:
                    for q in range(Q):
                        sp.wait_ge(S["e_mm"], H * q + H + i * RING)
                        sp.dma_start(chunk[:, q, :, 0:EA], rv[:, ds(i * RING + q * H, H), :]
                                     ).then_inc(S[f"ch{q}"], 16)
            with sp.Else():
                sp.sem_inc(S["rec2_in"], 16)
                full = (KT - 1) // H
                assert full * H == KT - 1
                gv = t["edge_attr_64"][0:full * H * P, :].rearrange("(g j p) f -> p g j f", j=H, p=P)

                def load(i, q):
                    sp.wait_ge(S["e_mm"], H * q + H + i * RING)
                    sp.dma_start(chunk[:, q, :, 0:EA], gv[:, ds(i * Q + q, 1), :, :].rearrange("p a j f -> p (a j) f")
                                 ).then_inc(S[f"ch{q}"], 16)

                with sp.Fori(0, full // Q) as i:
                    for q in range(Q):
                        load(i, q)
                for g in range(full // Q * Q, (NI - 1) * Q):
                    if g < full:
                        load(g // Q, g % Q)
                    elif g == full:
                        sp.wait_ge(S["e_mm"], H * g + H)
                        sp.dma_start(chunk[0:E - full * H * P, g % Q, 0, 0:EA], t["edge_attr_64"][full * H * P:E, :]
                                     ).then_inc(S[f"ch{g % Q}"], 16)
                    else:
                        sp.wait_ge(S["e_mm"], H * g + H)
                        sp.sem_inc(S[f"ch{g % Q}"], 16)
            sp.wait_ge(S["e_summed"], 1)
            sp.dma_start(e2_d, accT[:, 2:4, :].rearrange("p m n -> p (m n)")).then_inc(S["e2_out"], 16)
            sp.wait_ge(S["mm_done"], 4 * NG * SUMS)
            sp.wait_ge(S["e2_out"], 16)
            sp.dma_start(accT[:, 2:4, :].rearrange("p m n -> p (m n)"), e2_d).then_inc(S["e2_in"], 16)
            store_rows(1)
            sp.wait_ge(S["ev_done"], 4 + 4 * NG * (SUMS + 1))
            sp.wait_ge(S["e2_in"], 16)
            sp.dma_start(e2_d, accT[:, 2:4, :].rearrange("p m n -> p (m n)")).then_inc(S["e2_out"], 16)
            for u in range(2, AG - 1):
                store_rows(u)
            sp.wait_ge(S["mm_done"], 4 * NG * (2 * L + 2))
            sp.wait_ge(S["e2_out"], 32)
            sp.dma_start(accT[:, 2:4, :].rearrange("p m n -> p (m n)"), e2_d).then_inc(S["e2_in"], 16)
            with sp.Fori(0, NG) as g:
                sp.wait_ge(S["ln_act"], NB + 2 + G + g * G)
                sp.dma_start(hv[:, ds(g * G, G), :], stR).then_inc(S["m_h1"], 16)
                sp.wait_ge(S["stN_done"], NG * (AG - 1) + 1 + g)
                sp.dma_start(tv[:, ds(g * G, G), :], stN[:, :, :]).then_inc(S["tab_done"], 16)
            sp.wait_ge(S["m_h1"], 16 * NG)

            def mlp_rows(b, last):
                sp.wait_ge(S["m_y"], YC - 6 + b * 8)
                sp.wait_ge(S["agg_summed"], 1)
                sp.dma_start(h1b, h1_rows[ds(b * P, P), :]).then_inc(S["m_h1"], 16)
                sp.wait_ge(S["m_out"], b + 1)
                if last:
                    sp.dma_start(out[b * P:N, :], y[0:LASTR, :]).then_inc(S["m_st"], 16)
                else:
                    sp.dma_start(out[ds(b * P, P), :], y).then_inc(S["m_st"], 16)

            with sp.Fori(0, NB - 1) as b:
                mlp_rows(b, False)
            mlp_rows(NB - 1, True)
            sp.wait_ge(S["m_st"], 16 + 16 * NB)

        @block.gpsimd
        def _(pool):
            k = [0]

            def c(ins):
                k[0] += 1
                ins.then_inc(S["consts"], 1)
                pool.wait_ge(S["consts"], k[0])

            c(pool.iota(iota[:, :], [[1, P]], base=0, channel_multiplier=0, allow_small_or_imprecise_dtypes=True))
            c(pool.iota(blk128, [[P, NT]], base=0, channel_multiplier=0, allow_small_or_imprecise_dtypes=True))
            c(pool.memset(onesf[:, :], 1.0))
            c(pool.memset(onesb, 1.0))
            c(pool.memset(epsc[:, :], EPS))
            c(pool.affine_select(out=ident[:, :], in_=onesf[:, :], compare_op=ALU.is_equal, fill=0.0, base=0,
                                 pattern=[[1, P]], channel_multiplier=-1))
            c(pool.affine_select(out=Lm, in_=onesb, compare_op=ALU.is_gt, fill=0.0, base=0,
                                 pattern=[[1, EP]], channel_multiplier=-1))
            c(pool.memset(U, 1.0))
            c(pool.affine_select(out=U, in_=U, compare_op=ALU.is_gt, fill=0.0, base=0,
                                 pattern=[[-TC, CH], [1, ETP]], channel_multiplier=-1))
            c(pool.affine_select(out=U25[:, :], in_=onesf[0:NBP, 0:NBP], compare_op=ALU.is_gt, fill=0.0, base=0,
                                 pattern=[[1, NBP]], channel_multiplier=-1))
            c(pool.affine_select(out=V25[:, :], in_=onesf[0:NBP, 0:NBP], compare_op=ALU.is_ge, fill=0.0, base=0,
                                 pattern=[[1, NBP]], channel_multiplier=-1))
            halves = ((0, SCA), (SCA, SC))

            def scatter(rec, rd, h, done):
                for j in range(*halves[h]):
                    pool.indirect_dma_start(rd[:, :], bass.IndirectOffsetOnAxis(ap=rr1[:, j, 3:4].bitcast(I32), axis=0),
                                            rec[:, j, :], None).then_inc(S[done + "ab"[h]], 16)

            pool.wait_ge(S["filled1"], 16 * (NT // 44))
            pool.wait_ge(S["pos_done"], 1)
            for i0, n in ((0, 1), (1, STEPS - 1)):
                with pool.Fori(i0, i0 + n) as i:
                    for h, (lo, hi) in enumerate(halves):
                        if i0:
                            pool.wait_ge(S["scat_" + "ab"[h]], i * (16 * (hi - lo)))
                            pool.nop(nofuse=True)
                        pool.tensor_copy(rr1[:, lo:hi, :].bitcast(I32),
                                         meta[0][:, ds(i * SC + lo, hi - lo), :].bitcast(I32)
                                         ).then_inc(S["rec1_copied"], 1)
                        pool.wait_ge(S["rec1_copied"], 1 + h + i * 2)
                        pool.nop(nofuse=True)
                        scatter(rr1, rec1_d, h, "scat_")
            for h, (lo, hi) in enumerate(halves):
                pool.wait_ge(S["scat_" + "ab"[h]], 16 * (hi - lo) * STEPS)
            pool.dma_start(rec1[:, :, :], rec1_d.rearrange("(p t) f -> p t f", p=P)).then_inc(S["rec1_in"], 16)
            pool.wait_ge(S["flag_done"], 1)
            flag = pool.value_load(general[0:1, 0:1], min_val=0, max_val=1)
            with pool.If(flag):
                pool.wait_ge(S["filled2"], 16 * (NT // 44 + NI))
                pool.wait_ge(S["pos_done"], 2)
                for i0, n in ((0, 1), (1, STEPS - 1)):
                    with pool.Fori(i0, i0 + n) as i:
                        for h, (lo, hi) in enumerate(halves):
                            if i0:
                                pool.wait_ge(S["gscat_" + "ab"[h]], i * (32 * (hi - lo)))
                            pool.wait_ge(S["attr_" + "ab"[h]], 16 + i * 16)
                            pool.nop(nofuse=True)
                            pool.tensor_copy(rr1[:, lo:hi, :].bitcast(I32),
                                             meta[1][:, ds(i * SC + lo, hi - lo), :].bitcast(I32)
                                             ).then_inc(S["rec2_copied"], 1)
                            pool.wait_ge(S["rec2_copied"], 1 + h + i * 2)
                            pool.nop(nofuse=True)
                            scatter(rr1, rec3_d, h, "gscat_")
                            scatter(rr2, rec2_d, h, "gscat_")
            pool.wait_ge(S["rec1_in"], 16)
            pool.wait_ge(S["rec2_in"], 16)

            for a in range(AG):
                pool.wait_ge(S["tab_done"], rows_stored(0, a + 1) if a < AG - 1 else rows_stored(0, a) + 16 * NG)
                pool.wait_ge(S["tab_odd"], rows_stored(1, min(a + 1, AG - 1)))
                pool.wait_ge(S["self_done"], NG * (a + 1))
                def gathers(i):
                    for q in range(Q):
                        pool.wait_ge(S["agg_mm"], NT * a + H * q + H + i * RING)
                        idx = (rec1 if a < AG - 1 else rec2)[:, ds(i * RING + q * H, H), 0]
                        pool.nop(nofuse=True)
                        pool.tensor_copy(gidx[:, q * H:q * H + H], idx.bitcast(I32)).then_inc(S["idx_done"], 1)
                        pool.wait_ge(S["idx_done"], NI * Q * a + q + 1 + i * Q)
                        pool.nop(nofuse=True)
                        for j in range(q * H, q * H + H):
                            pool.indirect_dma_start(ring[:, j, :], None, table[:, :],
                                                    bass.IndirectOffsetOnAxis(ap=gidx[:, j:j + 1], axis=0)
                                                    ).then_inc(S[f"g{q}"], 16)

                if a < AG - 1:
                    with pool.Fori(0, NI) as i:
                        gathers(i)
                else:
                    tiles_in_order(pool, lambda i, last: gathers(i))

        @block.vector
        def _(dve):
            k = {"dve_c": 0, "dve_g": 0}

            def link(ins, name):
                k[name] += 1
                ins.then_inc(S[name], 1)
                dve.wait_ge(S[name], k[name])

            c = lambda ins: link(ins, "dve_c")

            dve.sem_inc(S["acc_done"], AC)
            dve.sem_inc(S["e_acc"], EB)
            dve.sem_inc(S["m_y"], YC)
            dve.sem_inc(S["m_st"], 16)
            dve.sem_inc(S["tab_done"], 16)
            dve.sem_inc(S["tab_odd"], 16)
            c(dve.memset(x_nm[:, NB - 1, :], 0.0))
            c(dve.memset(srci, 0))
            c(dve.memset(dsti, 0))
            c(dve.memset(nxt, 1 << 20))
            c(dve.memset(dstR, -1))
            c(dve.memset(srcR, 0))
            dve.memset(wgt, 0.0).then_inc(S["keys_done"], 1)
            c(dve.memset(fill1[:, :, :], 0.0))
            c(dve.memset(fill1[:, :, 1], -1.0))
            c(dve.memset(chunk[:, :, :, :], 0.0))
            c(dve.memset(chunk[:, :, :, EA], 1.0))
            c(dve.memset(bad[:, :], 0.0))
            c(dve.memset(rec2[:, :, 0].bitcast(I32), 0))
            c(dve.memset(rec2[:, :, 1], -1.0))
            dve.memset(blkoff[1][:, :], 0).then_inc(S["fills"], 1)
            dve.wait_ge(S["fills"], 1)
            dve.wait_ge(S["edges_in"], 48)
            dve.wait_ge(S["consts"], 11)

            def sort(s, arr, other, chain):
                c = lambda ins: link(ins, chain)
                m = meta[s]
                c(dve.tensor_scalar(keyi, arr, 7, None, ALU.arith_shift_right))
                c(dve.tensor_copy(keyf, keyi))
                c(dve.memset(keyf[:, ET:ETP], -1.0))
                if s:
                    dve.wait_ge(S["cnt_done"], KA)
                for b in range(NBP):
                    dve.tensor_scalar(OH[:, b, :], keyf, float(b), None, ALU.is_equal).then_inc(S["hots_done"], 1)
                c(dve.tensor_scalar(low, arr, P - 1, None, ALU.bitwise_and))
                c(dve.tensor_copy(m[:, :, 1], low))
                c(dve.tensor_copy(m[:, :, 0].bitcast(I32), other))
                c(dve.tensor_copy(m[:, :, 2], wgt))
                dve.wait_ge(S["hots_done"], NBP * (s + 1))
                dve.tensor_reduce(cnt[:, KA:NBP], OH[:, KA:NBP, 0:ET], AX.X, ALU.add).then_inc(S["cnt_rest"], 1)
                dve.wait_ge(S["totb_done"], s + 1)
                c(dve.tensor_copy(padi[:, :], bank[0][0:NBP, 0:P]))
                c(dve.tensor_scalar(padi[:, :], padi[:, :], P - 1, None, ALU.add))
                c(dve.tensor_scalar(padi[:, :], padi[:, :], 7, None, ALU.arith_shift_right))
                dve.tensor_scalar(padf[:, :], padi[:, :], float(P), None, ALU.mult).then_inc(S["pad_done"], 1)
                dve.wait_ge(S["starts_done"], s + 1)
                c(dve.tensor_copy(start[:, :], bank[1][:, 0:NBP]))
                c(dve.tensor_copy(end[:, :], bank[2][0:NBP, 0:1]))
                dve.tensor_scalar(ended, blk128, end[:, 0:1], None, ALU.is_ge).then_inc(S["ended_done"], 1)
                c(dve.memset(posf, 0.0))
                for b in range(NBP + 1):
                    if b < NBP:
                        dve.wait_ge(S["sort_pe_r"], NBP * s + b + 1)
                        if b >= 2:
                            dve.wait_ge(S["pos_sum"], NBP * s + b - 1)
                        dve.scalar_tensor_tensor(term[b % 2], bank[6 + b % 2][0:EP, 0:ETP], start[0:EP, b:b + 1],
                                                 OH[:, b, :], ALU.add, ALU.mult).then_inc(S["sort_dve_r"], 1)
                    if b:
                        dve.wait_ge(S["sort_dve_r"], NBP * s + b)
                        if b > 1:
                            dve.wait_ge(S["pos_sum"], NBP * s + b - 1)
                        dve.tensor_tensor(posf, posf, term[(b - 1) % 2], ALU.add).then_inc(S["pos_sum"], 1)
                dve.wait_ge(S["pos_sum"], NBP * (s + 1))
                c(dve.tensor_copy(keyi, posf))
                c(dve.tensor_scalar(low, keyi, P - 1, None, ALU.bitwise_and))
                c(dve.tensor_scalar(keyi, keyi, 7, None, ALU.arith_shift_right))
                dve.scalar_tensor_tensor(m[:, :, 3].bitcast(I32), low, float(NT), keyi, ALU.mult, ALU.add
                                         ).then_inc(S["pos_done"], 1)
                dve.wait_ge(S["blk_done"], s + 1)
                c(dve.tensor_scalar(blkoff[s][:, :], bank[3][0:1, 0:NT], float(NB - 1), float(P), ALU.min, ALU.mult))
                dve.wait_ge(S["pos_done"], s + 1)

            sort(0, srci, dsti, "dve_c")
            dve.wait_ge(S["rows_in"], 16 * (2 + 2 * (KC + 1)))
            c(dve.tensor_copy(keyf[:, 0:ET], dsti[:, 0:ET]))
            c(dve.tensor_copy(posf[:, 0:ET], nxt[:, 0:ET]))
            c(dve.tensor_tensor(term[0][:, 0:ET], keyf[:, 0:ET], posf[:, 0:ET], ALU.is_gt))
            c(dve.tensor_reduce(bad[0:EP, KC:KC + 1], term[0][:, 0:ET], AX.X, ALU.add))
            c(dve.tensor_copy(dstF, dstR))
            c(dve.tensor_copy(srcF, srcR))
            c(dve.tensor_scalar(first[:, :], dstF[:, :, 0], float(WIN), None, ALU.min))
            for q in range(KC):
                c(dve.tensor_scalar(dstF[:, q, :], dstF[:, q, :], first[:, q:q + 1], None, ALU.subtract))
            c(dve.tensor_reduce(bad[0:KR, 0:KC], dstF, AX.X, ALU.max))
            dve.tensor_scalar(bad[0:KR, 0:KC], bad[0:KR, 0:KC], float(P - 1), None, ALU.is_gt
                              ).then_inc(S["rows_done"], 1)
            dve.wait_ge(S["rows_turned"], 1)
            c(dve.tensor_copy(rec2[:, 0:KT, 1], bank[0][:, 0:KT]))
            c(dve.tensor_copy(rec2[:, 0:KT, 0].bitcast(I32), bank[1][:, 0:KT]))
            c(dve.tensor_copy(blkoff[1][:, 0:KT], bank[2][0:1, 0:KT]))
            c(dve.tensor_reduce(bad[0:1, 0:1], bank[3][0:1, 0:KC + 1], AX.X, ALU.add))
            dve.tensor_scalar(general[:, :], bad[0:1, 0:1], 0.0, None, ALU.is_gt).then_inc(S["flag_done"], 1)
            dve.wait_ge(S["flag_done"], 1)
            flag = dve.value_load(general[0:1, 0:1], min_val=0, max_val=1)
            with dve.If(flag):
                sort(1, dsti, srci, "dve_g")

            def group_stats(r, g):
                for j in range(G):
                    dve.bn_stats(st[:, ds(g * G + j, 1), :], x_nm[:, ds(g * G + j, 1), :]).then_inc(S["ln_dve"], 1)

            def row_scales(r):
                dve.wait_ge(S["ln_dve"], (2 * r + 1) * NB + r)
                for b in range(NB):
                    dve.bn_aggr(mv[:, b, :], st[:, b, :]).then_inc(S["ln_dve"], 1)
                dve.wait_ge(S["ln_act"], r * (NB + 1) + 1)
                c(dve.reciprocal(rs[:, :], sd[:, :]))
                dve.scalar_tensor_tensor(nb[:, :], mv[:, :, 0], -1.0, rs[:, :], ALU.mult, ALU.mult
                                         ).then_inc(S["ln_dve"], 1)

            dve.wait_ge(S["x_in"], 32)
            with dve.Fori(0, NG) as g:
                group_stats(0, g)
            row_scales(0)
            pT = [bank[4], bank[5]]
            with dve.Fori(0, NG) as g:
                for m in range(DH):
                    for hh in range(2):
                        n = 3 if hh == 0 else 2
                        dve.wait_ge(S["tr_done"], m * 2 + hh + 1 + g * 4)
                        dve.tensor_copy(accT[:, 2 + m, ds(g * GC + hh * 3 * P, n * P)], bank[4 + m * 2 + hh][:, 0:n * P]
                                        ).then_inc(S["ev_T"], 1)

            def rows_from_columns(u):
                for g in range(NG):
                    dest = (stN[:, :, :], stR)[g % 2]
                    dve.wait_ge(S[("tab_done", "tab_odd")[g % 2]], rows_stored(g % 2, u) + g // 2 * 16)
                    for q in range(3):
                        n = 2 if q < 2 else 1
                        dve.wait_ge(S["tr_done"], 4 * NG + u * 3 * NG + q + 1 + g * 3)
                        dve.tensor_copy(dest[:, 2 * q:2 * q + n, :], bank[4 + q][:, 0:n * D]
                                        .rearrange("p (b f) -> p b f", f=D)).then_inc(S["ev_T"], 1)
                    dve.wait_ge(S["ev_T"], 4 * NG + u * 3 * NG + 3 + g * 3)
                    dve.sem_inc(S["stN_done"], 1)

            def rows_added():
                u = L
                with dve.Fori(0, NG) as g:
                    for q in range(3):
                        n = 2 if q < 2 else 1
                        dve.wait_ge(S["tr_done"], 4 * NG + u * 3 * NG + q + 1 + g * 3)
                        xs = x_nm[:, ds(g * G + 2 * q, n), :]
                        dve.tensor_tensor(xs, xs, bank[4 + q][:, 0:n * D].rearrange("p (b f) -> p b f", f=D),
                                          ALU.add).then_inc(S["ev_T"], 1)
                    dve.wait_ge(S["ev_T"], 4 * NG + u * 3 * NG + 3 + g * 3)
                    group_stats(1, g)

            def accumulate(a):
                edges = a is None
                first_layer = not edges and a < AG - 1
                t0 = 0 if edges else NT * a
                hots, mm, acc = ("e_hot", "e_mm", "e_acc") if edges else ("hot_done", "agg_mm", "acc_done")
                banks, granted, row = ((0, 1, 6, 7), EB, 2) if edges else (range(H), AC, 0)
                offsets = blkoff[0] if first_layer else blkoff[1]

                def one_hot(i, j):
                    q = j // H
                    if j % H == 0:
                        dve.wait_ge(S[mm], t0 + (q + 1) * H - HOT + CR + i * RING)
                    if first_layer:
                        r = rec1[:, ds(i * RING + j, 1), :]
                        ins = dve.tensor_scalar(hot[:, j % HOT, :], iota[:, :], r[:, 0, 1:2], r[:, 0, 2:3],
                                                ALU.is_equal, ALU.mult)
                    else:
                        ins = dve.tensor_scalar(hot[:, j % HOT, :], iota[:, :], rec2[:, ds(i * RING + j, 1), 1], None,
                                                ALU.is_equal)
                    ins.then_inc(S[hots], 1)

                def first_columns(i, j):
                    return nc.values_load_multi_w_load_instructions(
                        offsets[0:1, ds(i * RING + j, H)], engines=[mybir.EngineType.DVE],
                        min_val=0, max_val=WIN)[1]

                def add(i, j, off):
                    dve.wait_ge(S[mm], t0 + CR + j + 1 + i * RING)
                    dve.wait_ge(S[acc], t0 + granted + j + i * RING)
                    tgt = accT[:, row:row + 2, ds(off, P)]
                    dve.tensor_tensor(tgt, tgt, bank[banks[j % len(banks)]][:, 0:D].rearrange("p (w n) -> p w n", w=2),
                                      ALU.add).then_inc(S[acc], 1)

                for j in range(H):
                    one_hot(0, j)
                def ring_of_adds(i, last):
                    for j in range(RING):
                        if not last or j + H < RING:
                            one_hot(i + (j + H) // RING, (j + H) % RING)
                        if j % H == 0:
                            offs = first_columns(i, j)
                        add(i, j, offs[j % H])
                    if last:
                        dve.wait_ge(S[acc], t0 + granted + RING + i * RING)

                if first_layer:
                    with dve.Fori(0, NI - 1) as i:
                        ring_of_adds(i, False)
                    ring_of_adds(NI - 1, True)
                else:
                    tiles_in_order(dve, ring_of_adds)
                    dve.sem_inc(S["e_summed" if edges else "agg_summed"], 1)

            def batch_stats(d, buf, gamma, beta, l):
                base = 4 + 4 * NG * (first_linear_of(l) + d % 2)
                for g0, n in ((0, NG - 1), (NG - 1, 1)):
                    with dve.Fori(g0, g0 + n) as g:
                        for m in range(DH):
                            for hh in range(2):
                                dve.wait_ge(S["ev_done"], base + m * 2 + hh + 1 + g * 4)
                                w = HC if g0 == 0 else min(HC, N - (NG - 1) * GC - hh * HC)
                                dve.bn_stats(bst[:, m, ds(g * 2 + hh, 1), :],
                                             accT[:, buf + m, ds(g * GC + hh * HC, w)]).then_inc(S["bn_stat"], 1)
                dve.wait_ge(S["bn_stat"], 4 * NG * (d + 1) + 2 * d)
                for m in range(DH):
                    dve.bn_aggr(bmv[:, m, :], bst[:, m, :, :].rearrange("p a b -> p (a b)")).then_inc(S["bn_stat"], 1)
                dve.wait_ge(S["bn_sd"], d + 1)
                c(dve.reciprocal(brs[:, :], bsd[:, :]))
                lo = slice(l * DH, l * DH + DH)
                c(dve.tensor_tensor(bsc[:, :], brs[:, :], vec[gamma][:, lo], ALU.mult))
                c(dve.tensor_tensor(bms[:, :], bmv[:, :, 0], bsc[:, :], ALU.mult))
                dve.tensor_tensor(bbi[:, :], vec[beta][:, lo], bms[:, :], ALU.subtract).then_inc(S["bn_dve"], 1)

            dve.wait_ge(S["vec_in"], 16 * (len(COLS) + 4 + len(rows) - len(LATE) + 1))
            rows_from_columns(0)
            dve.wait_ge(S["mm_done"], 4 * NG)
            c(dve.memset(accT[:, 2:4, :], 0.0))
            for m in range(DH):
                c(dve.tensor_scalar(accT[:, 2 + m, :], accT[:, 2 + m, :], vec["L1_gnn_ee_b1"][:, m:m + 1], 0.0,
                                    ALU.add, ALU.max))
            dve.wait_ge(S["rec2_in"], 16)
            accumulate(None)
            for l in range(L):
                dve.wait_ge(S["self_done"], NG * (l + 1))
                if l == 0:
                    dve.wait_ge(S["rec1_in"], 16)
                accumulate(l)
                batch_stats(2 * l, 2, "L0_gnn_g1", "L0_gnn_be1", l)
                batch_stats(2 * l + 1, 0, "L0_gnn_g_out", "L0_gnn_b_out", l)
                if l < L - 1:
                    rows_from_columns(l + 1)
                else:
                    rows_added()
            row_scales(1)
            c(dve.tensor_scalar(eps2[:, :], epsv[:, :], 2.0, None, ALU.add))
            dve.wait_ge(S["e2_in"], 32)
            with dve.Fori(0, NG) as g:
                for j in range(G):
                    if j == 0:
                        dve.wait_ge(S["tab_done"], rows_stored(0, AG - 1) + g * 16)
                    dve.wait_ge(S["ln_act"], (NB + 1) + 1 + j + 1 + g * G)
                    dve.tensor_tensor(stN[:, j, :], stF[:, j * D:j * D + D],
                                      rows["L1_gnn_ee_b2"][:, :], ALU.add).then_inc(S["init_done"], 1)
                dve.wait_ge(S["init_done"], G + g * G)
                dve.sem_inc(S["stN_done"], 1)
                for m in range(DH):
                    for hh in range(2):
                        n = 3 if hh == 0 else 2
                        dve.wait_ge(S["tr_done"], 4 * NG + 3 * NG * AG + m * 2 + hh + 1 + g * 4)
                        cols = ds(g * GC + hh * 3 * P, n * P)
                        dve.scalar_tensor_tensor(accT[:, m, cols], bank[4 + m * 2 + hh][:, 0:n * P], eps2[:, 0:1],
                                                 accT[:, 2 + m, cols], ALU.mult, ALU.add).then_inc(S["ev_T"], 1)
                dve.wait_ge(S["ev_T"], 4 * NG + 3 * NG * AG + 4 + g * 4)
                dve.sem_inc(S["self_done"], 1)
            accumulate(AG - 1)
            def mlp_norm(s, b):
                mm, zz = ("m_mm1", "m_mm2")[s], ("m_z1", "m_z2")[s]
                dve.wait_ge(S[mm], 1 + b)
                for q in range(2):
                    dve.tensor_tensor(z[s][:, q * 512:q * 512 + 512], bank[(0, 4)[s] + q][:, :],
                                      rows[("L1_gnn_b1", "L1_gnn_b2")[s]][:, q * 512:q * 512 + 512], ALU.add
                                      ).then_inc(S[zz], 1)
                dve.wait_ge(S[zz], 2 + b * 5)
                for q in range(2):
                    dve.bn_stats(mst[s][:, q, :], z[s][:, q * 512:q * 512 + 512]).then_inc(S[zz], 1)
                dve.wait_ge(S[zz], 4 + b * 5)
                dve.nop(nofuse=True)
                dve.bn_aggr(mmv[s][:, :], mst[s][:, :, :].rearrange("p a b -> p (a b)")).then_inc(S[zz], 1)
                dve.wait_ge(S[("m_sd1", "m_sd2")[s]], 1 + b)
                dve.reciprocal(mrs[s][:, :], msd[s][:, :]).then_inc(S[("m_rs1", "m_rs2")[s]], 1)
                dve.wait_ge(S[("m_rs1", "m_rs2")[s]], 1 + b)
                dve.scalar_tensor_tensor(mnb[s][:, :], mmv[s][:, 0:1], -1.0, mrs[s][:, :], ALU.mult, ALU.mult
                                         ).then_inc(S[("m_n1", "m_n2")[s]], 1)

            def mlp_result(b):
                dve.wait_ge(S["m_mm3"], 1 + b)
                dve.wait_ge(S["m_st"], 16 + b * 16)
                dve.tensor_tensor(y, bank[6][:, 0:D], rows["L1_gnn_b3"], ALU.add).then_inc(S["m_y"], 1)
                dve.wait_ge(S["m_h1"], 16 * NG + 16 + b * 16)
                dve.wait_ge(S["m_y"], YC + 1 + b * 8)
                dve.tensor_tensor(y, y, h1b, ALU.add).then_inc(S["m_y"], 1)
                dve.wait_ge(S["m_y"], YC + 2 + b * 8)
                dve.bn_stats(yst[:, :], y).then_inc(S["m_y"], 1)
                dve.wait_ge(S["m_y"], YC + 3 + b * 8)
                dve.nop(nofuse=True)
                dve.bn_aggr(ymv[:, :], yst[:, :]).then_inc(S["m_y"], 1)
                dve.wait_ge(S["m_sdy"], 1 + b)
                dve.reciprocal(yrs[:, :], ysd[:, :]).then_inc(S["m_y"], 1)
                dve.wait_ge(S["m_y"], YC + 5 + b * 8)
                dve.tensor_scalar(y, y, ymv[:, 0:1], yrs[:, 0:1], ALU.subtract, ALU.mult).then_inc(S["m_y"], 1)
                dve.wait_ge(S["m_y"], YC + 6 + b * 8)
                dve.tensor_tensor(y, y, rows["L1_gnn_bn_g"], ALU.mult).then_inc(S["m_y"], 1)
                dve.wait_ge(S["m_y"], YC + 7 + b * 8)
                dve.tensor_tensor(y, y, rows["L1_gnn_bn_b"][:, :], ALU.add).then_inc(S["m_y"], 1)
                dve.wait_ge(S["m_y"], YC + 8 + b * 8)
                dve.scalar_tensor_tensor(y, y, 0.0, x_nm[:, ds(b, 1), :].rearrange("p a f -> p (a f)"), ALU.max,
                                         ALU.add).then_inc(S["m_out"], 1)

            dve.wait_ge(S["late_in"], 16 * len(LATE))
            skewed(dve, ((1, lambda b: mlp_norm(0, b)), (-2, mlp_result), (0, lambda b: mlp_norm(1, b))))

        @block.scalar
        def _(act):
            act.sem_inc(S["ev_done"], 4)
            act.sem_inc(S["aT_done"], 2)
            act.sem_inc(S["emb_done"], 2)

            def sort(s):
                for b in range(KA):
                    act.wait_ge(S["hots_done"], NBP * s + b + 1)
                    if b:
                        act.wait_ge(S["cnt_done"], KA * s + b)
                    elif s:
                        act.wait_ge(S["totb_done"], 1)
                    act.activation(junk, OH[:, b, :], ACT.Identity, accum_out=cnt[:, b:b + 1]
                                   ).then_inc(S["cnt_done"], 1)
                with act.Fori(0, NBP // 2) as i:
                    for r in range(2):
                        act.wait_ge(S["sort_pe_t"], NBP * s + r + 1 + i * 2)
                        act.copy(tot[:, r, :, :].rearrange("p c m -> p (c m)"), bank[4 + r][0:TC, 0:CH * EP]
                                 ).then_inc(S["sort_act_t"], 1)

            sort(0)
            act.wait_ge(S["flag_done"], 1)
            flag = act.value_load(general[0:1, 0:1], min_val=0, max_val=1)
            with act.If(flag):
                sort(1)

            def ln_rows(r):
                act.wait_ge(S["ln_dve"], 2 * NB * (r + 1) + r)
                act.activation(sd[:, :], mv[:, :, 1], ACT.Sqrt, bias=epsc[:, 0:1]).then_inc(S["ln_act"], 1)
                act.wait_ge(S["ln_dve"], (2 * NB + 1) * (r + 1))
                if r:
                    act.wait_ge(S["tab_odd"], rows_stored(1, AG - 1))
                with act.Fori(0, NG) as g:
                    for j in range(G):
                        if r and j == 0:
                            act.wait_ge(S["stT_free"], 1 + g)
                        act.activation(stF[:, j * D:j * D + D] if r else all_rows[:, ds(g * GC * DH + j * D, D)], x_nm[:, ds(g * G + j, 1), :], ACT.Relu,
                                       bias=nb[:, ds(g * G + j, 1)], scale=rs[:, ds(g * G + j, 1)]
                                       ).then_inc(S["ln_act"], 1)

            def evacuate(d, buf, name, l):
                with act.Fori(0, NG) as g:
                    for m in range(DH):
                        for hh in range(2):
                            q = m * 2 + hh
                            act.wait_ge(S["mm_done"], 4 * NG * d + q + 1 + g * 4)
                            act.activation(accT[:, buf + m, ds(g * GC + hh * HC, HC)], bank[q][:, 0:HC], ACT.Identity,
                                           bias=vec[name][:, l * DH + m:l * DH + m + 1]).then_inc(S["ev_done"], 1)

            def to_stage(u):
                with act.Fori(0, NG) as g:
                    for m in range(DH):
                        src, dest = accT[:, m, ds(g * GC, GC)], all_cols[:, m, ds(g * GC, GC)]
                        if u:
                            act.activation(dest, src, ACT.Relu, bias=bbi[:, m:m + 1], scale=bsc[:, m:m + 1]
                                           ).then_inc(S["st_done"], 1)
                        else:
                            act.copy(dest, src).then_inc(S["st_done"], 1)
                act.wait_ge(S["st_done"], 2 * NG * (u + 1))
                if 0 < u < L:
                    with act.Fori(0, NG) as g:
                        for m in range(DH):
                            act.copy(accT[:, m, ds(g * GC, GC)], all_cols[:, m, ds(g * GC, GC)]
                                     ).then_inc(S["app_done"], 1)
                    act.wait_ge(S["app_done"], 4 * NG * u)
                act.sem_inc(S["self_done"], NG)

            def bn_sd(d):
                act.wait_ge(S["bn_stat"], (4 * NG + 2) * (d + 1))
                act.activation(bsd[:, :], bmv[:, :, 1], ACT.Sqrt, bias=epsc[:, 0:1]).then_inc(S["bn_sd"], 1)

            act.wait_ge(S["consts"], 11)
            act.wait_ge(S["x_in"], 32)
            ln_rows(0)
            act.wait_ge(S["vec_in"], 16 * (len(COLS) + 4 + len(rows) - len(LATE) + 1))
            evacuate(0, 0, "L0_gnn_b_in", 0)
            act.wait_ge(S["ev_done"], 4 + 4 * NG)
            to_stage(0)
            def copy_turned(i, j):
                act.wait_ge(S["tr2_done"], j + 1 + i * RING)
                act.wait_ge(S["r_done"], j + 1 + i * RING)
                act.copy(aT[:, j % 2, :], bank[2 + j % 2][0:EA + 1, 0:P]).then_inc(S["aT_done"], 1)

            def embed(i, j):
                act.wait_ge(S["r_done"], 2 + j + 1 + i * RING)
                act.wait_ge(S["e_mm"], CR - EB + j + 1 + i * RING)
                act.activation(emb[:, j % EB, :], bank[4 + j % 2][:, 0:D], ACT.Relu).then_inc(S["emb_done"], 1)

            copy_turned(0, 0)
            def ring_of_embeddings(i, last):
                for j in range(RING):
                    if not last or j + 1 < RING:
                        copy_turned(i + (j + 1) // RING, (j + 1) % RING)
                    embed(i, j)

            tiles_in_order(act, ring_of_embeddings)
            act.wait_ge(S["e2_out"], 16)
            for l in range(L):
                evacuate(first_linear_of(l), 2, "L0_gnn_b1", l)
                bn_sd(2 * l)
                act.wait_ge(S["bn_dve"], 2 * l + 1)
                with act.Fori(0, NG) as g:
                    for m in range(DH):
                        sl = accT[:, 2 + m, ds(g * GC, GC)]
                        act.activation(sl, sl, ACT.Relu, bias=bbi[:, m:m + 1], scale=bsc[:, m:m + 1]
                                       ).then_inc(S["app_done"], 1)
                evacuate(first_linear_of(l) + 1, 0, "L0_gnn_b2", l)
                bn_sd(2 * l + 1)
                act.wait_ge(S["bn_dve"], 2 * l + 2)
                to_stage(l + 1)
                if l == 0:
                    with act.Fori(0, NG) as g:
                        act.wait_ge(S["mm_done"], 4 * NG * SUMS + 4 + g * 4)
                        for m in range(DH):
                            for hh in range(2):
                                act.activation(accT[:, 2 + m, ds(g * GC + hh * HC, HC)], bank[m * 2 + hh][:, 0:HC],
                                               ACT.Identity, bias=vec["L1_gnn_ee_b2"][:, m:m + 1]).then_inc(S["ev_done"], 1)
                    act.wait_ge(S["e2_out"], 32)
            ln_rows(1)
            act.wait_ge(S["acc_done"], AC + NT * (AG - 1))
            for n in LATE:
                act.dma_start(rows[n], t[n].partition_broadcast(P)).then_inc(S["late_in"], 16)
            pieces = [(w1, "L1_gnn_w1", k) for k in range(DH)] + [(w2, "L1_gnn_w2", k) for k in range(KH)] + \
                     [(w3, "L1_gnn_w3", slice(0, KH))]
            for i, (dest, n, k) in enumerate(pieces):
                act.wait_ge(S["acc_done"], AC + NT * (AG - 1) + (i + 1) * RING)
                act.dma_start(dest[:, k], dram_T(t[n], dest.shape[1])[:, k]).then_inc(S["wl1_in"], 16)

            def block_columns(b):
                if not isinstance(b, int) or b:
                    act.wait_ge(S["m_mm1"], b)
                act.nop(nofuse=True)
                for m in range(DH):
                    act.copy(hblk[:, m, :], accT[:, m, ds(b * P, P)]).then_inc(S["m_blk"], 1)

            def normalise(s, b):
                act.wait_ge(S[("m_z1", "m_z2")[s]], 5 + b * 5)
                act.activation(msd[s][:, :], mmv[s][:, 1:2], ACT.Sqrt, bias=epsc[:, 0:1]
                               ).then_inc(S[("m_sd1", "m_sd2")[s]], 1)
                act.wait_ge(S[("m_n1", "m_n2")[s]], 1 + b)
                act.activation(z[s], z[s], ACT.Identity, bias=mnb[s][:, 0:1], scale=mrs[s][:, 0:1]
                               ).then_inc(S[("m_nz1", "m_nz2")[s]], 1)

            def turned(s, b):
                for kk in range(KH):
                    act.wait_ge(S[("m_t1", "m_t2")[s]], kk // 4 + 1 + b * 2)
                    act.activation(zT[s][:, kk, :], bank[2 + kk // 4][:, kk % 4 * P:kk % 4 * P + P], ACT.Relu,
                                   bias=mvec[("L1_gnn_be1", "L1_gnn_be2")[s]][:, kk:kk + 1],
                                   scale=mvec[("L1_gnn_g1", "L1_gnn_g2")[s]][:, kk:kk + 1]
                                   ).then_inc(S[("m_a1", "m_a2")[s]], 1)

            def result_deviation(b):
                act.wait_ge(S["m_y"], YC + 4 + b * 8)
                act.activation(ysd[:, :], ymv[:, 1:2], ACT.Sqrt, bias=epsc[:, 0:1]).then_inc(S["m_sdy"], 1)

            act.wait_ge(S["agg_summed"], 1)
            skewed(act, ((1, lambda b: normalise(0, b)), (2, block_columns), (-1, lambda b: turned(1, b)),
                         (-2, result_deviation), (1, lambda b: turned(0, b)), (0, lambda b: normalise(1, b))))

        @block.tensor
        def _(pe):
            pe.sem_inc(S["agg_mm"], CR)
            pe.sem_inc(S["e_mm"], CR)
            pe.sem_inc(S["stT_free"], 1)
            pe.sem_inc(S["r_done"], 2)
            pe.wait_ge(S["consts"], 11)

            def sort(s):
                pe.wait_ge(S["cnt_done"], KA * (s + 1))
                pe.wait_ge(S["cnt_rest"], s + 1)
                pe.matmul(bank[0][0:NBP, 0:P], cnt[:, :], onesf[0:EP, :], start=True, stop=True).then_inc(S["totb_done"], 1)

                def column_sums(b, r, first=False):
                    if not first:
                        pe.wait_ge(S["sort_act_t"], NBP * s + b - 1)
                    for c in range(CH):
                        ins = pe.matmul(bank[4 + r][0:TC, c * EP:(c + 1) * EP], OH[:, ds(b, 1), c * TC:(c + 1) * TC]
                                        .rearrange("p a t -> p (a t)"), onesb, start=True, stop=True)
                    ins.then_inc(S["sort_pe_t"], 1)

                def ranks(b, r, first=False):
                    if not first:
                        pe.wait_ge(S["sort_dve_r"], NBP * s + b - 1)
                    pe.matmul(bank[6 + r][0:EP, 0:ETP], Lm, OH[:, ds(b, 1), :], start=True, stop=False)
                    pe.wait_ge(S["sort_act_t"], NBP * s + b + 1)
                    for c in range(CH):
                        ins = pe.matmul(bank[6 + r][0:EP, 0:ETP], tot[:, r, c, :], U[:, c, :], start=False,
                                        stop=c == CH - 1)
                    ins.then_inc(S["sort_pe_r"], 1)

                if s:
                    pe.wait_ge(S["pos_done"], 1)
                column_sums(0, 0, True)
                column_sums(1, 1, True)
                pe.wait_ge(S["pad_done"], s + 1)
                pe.matmul(bank[1][:, 0:NBP], padf[:, :], U25[:, :], start=True, stop=True)
                pe.matmul(bank[2][0:NBP, 0:1], V25[:, :], padf[:, 0:1], start=True, stop=True).then_inc(S["starts_done"], 1)
                ranks(0, 0, True)
                pe.wait_ge(S["ended_done"], s + 1)
                pe.matmul(bank[3][0:1, 0:NT], onesf[0:NBP, 0:1], ended, start=True, stop=True).then_inc(S["blk_done"], 1)
                column_sums(2, 0)
                ranks(1, 1, True)
                column_sums(3, 1)
                with pe.Fori(1, NBP // 2 - 1) as i:
                    for r in range(2):
                        ranks(i * 2 + r, r)
                        column_sums(i * 2 + 2 + r, r)
                for b in (NBP - 2, NBP - 1):
                    ranks(b, b % 2)
                pe.wait_ge(S["sort_dve_r"], NBP * (s + 1))

            sort(0)
            pe.wait_ge(S["rows_done"], 1)
            for c in range(KC):
                pe.transpose(bank[0][:, c * KR:(c + 1) * KR], dstF[:, c, :], ident[0:KR, 0:KR])
                pe.transpose(bank[1][:, c * KR:(c + 1) * KR], srcF[:, c, :], ident[0:KR, 0:KR])
                pe.matmul(bank[2][0:1, c * KR:(c + 1) * KR], first[:, c:c + 1], ident[0:KR, 0:KR], start=True, stop=True)
            pe.matmul(bank[3][0:1, 0:KC + 1], onesf[:, 0:1], bad[:, :], start=True, stop=True
                      ).then_inc(S["rows_turned"], 1)
            pe.wait_ge(S["flag_done"], 1)
            flag = pe.value_load(general[0:1, 0:1], min_val=0, max_val=1)
            with pe.If(flag):
                sort(1)

            def turn_rows(rows5, m, hh):
                for j in range(3 - hh):
                    jj = hh * 3 + j
                    ins = pe.transpose(bank[4 + m * 2 + hh][:, j * P:j * P + P],
                                       rows5[:, jj * D + m * P:jj * D + m * P + P], ident[:, :])
                ins.then_inc(S["tr_done"], 1)

            def turn_columns(cols5, q):
                for j in range(2 * q, min(2 * q + 2, G)):
                    for m in range(DH):
                        o = (j - 2 * q) * D + m * P
                        ins = pe.transpose(bank[4 + q][:, o:o + P], cols5[:, m, j * P:j * P + P], ident[:, :])
                ins.then_inc(S["tr_done"], 1)

            def first_rows_to_columns():
                for g in range(NG):
                    pe.wait_ge(S["ln_act"], 1 + G + g * G)
                    for m in range(DH):
                        for hh in range(2):
                            if g:
                                pe.wait_ge(S["ev_T"], g * 4 - 4 + m * 2 + hh + 1)
                            turn_rows(all_rows[:, g * G * D:(g + 1) * G * D], m, hh)

            def last_rows_to_columns():
                base = 4 * NG + 3 * NG * AG
                with pe.Fori(0, NG) as g:
                    pe.wait_ge(S["ln_act"], NB + 2 + G + g * G)
                    pe.wait_ge(S["ev_T"], base + g * 4)
                    for m in range(DH):
                        for hh in range(2):
                            turn_rows(stF, m, hh)
                    pe.wait_ge(S["m_h1"], 16 + g * 16)
                    pe.wait_ge(S["init_done"], G + g * G)
                    pe.wait_ge(S["tr_done"], base + 4 + g * 4)
                    pe.sem_inc(S["stT_free"], 1)

            def linear(d, lhs, buf, ready=None):
                with pe.Fori(0, NG) as g:
                    if ready:
                        pe.wait_ge(S[ready[0]], ready[1] + g * ready[2])
                    for m in range(DH):
                        for hh in range(2):
                            q = m * 2 + hh
                            pe.wait_ge(S["ev_done"], 4 * NG * d + q + 1 + g * 4)
                            for kk in range(DH):
                                ins = pe.matmul(bank[q][:, 0:HC], lhs[:, kk, m * P:m * P + P],
                                                accT[:, buf + kk, ds(g * GC + hh * HC, HC)], start=kk == 0,
                                                stop=kk == DH - 1)
                            ins.then_inc(S["mm_done"], 1)

            def columns_to_rows(u):
                for g in range(NG):
                    pe.wait_ge(S["st_done"], 2 * NG * u + 2 + g * 2)
                    for q in range(3):
                        pe.wait_ge(S["ev_T"], 4 * NG + 3 * NG * u + (g * 3 - 3 + q + 1 if g else 0))
                        turn_columns(all_cols[:, :, g * GC:(g + 1) * GC], q)

            def one_hot_products(a):
                def ring_of_products(i, last=False):
                    for j in range(RING):
                        if j % H == 0:
                            pe.wait_ge(S[f"g{j // H}"], 16 * H * (NI * a + 1) + i * (16 * H))
                        pe.wait_ge(S["hot_done"], NT * a + j + 1 + i * RING)
                        pe.wait_ge(S["acc_done"], NT * a + j - H + 1 + AC + i * RING)
                        for w in range(DH):
                            ins = pe.matmul(bank[j % H][:, w * P:w * P + P], ring[:, j, w * P:w * P + P],
                                            hot[:, j % HOT, :], start=True, stop=True)
                        ins.then_inc(S["agg_mm"], 1)

                if a < AG - 1:
                    with pe.Fori(0, NI) as i:
                        ring_of_products(i)
                else:
                    tiles_in_order(pe, ring_of_products)

            def edge_embeddings():
                def turn_attributes(i, j):
                    if j % H == 0:
                        pe.wait_ge(S[f"ch{j // H}"], 16 + i * 16)
                    pe.wait_ge(S["aT_done"], j + 1 + i * RING)
                    pe.transpose(bank[2 + j % 2][0:EA + 1, 0:P], chunk[:, j // H, j % H, :],
                                 ident[:, :]).then_inc(S["tr2_done"], 1)

                def first_linear(i, j):
                    pe.wait_ge(S["aT_done"], 2 + j + 1 + i * RING)
                    pe.wait_ge(S["emb_done"], j + 1 + i * RING)
                    pe.matmul(bank[4 + j % 2][:, 0:D], aT[:, j % 2, :], ee1[:, :], start=True, stop=True
                              ).then_inc(S["r_done"], 1)

                def products(i, j):
                    pe.wait_ge(S["e_hot"], j + 1 + i * RING)
                    pe.wait_ge(S["e_acc"], j + 1 + i * RING)
                    pe.wait_ge(S["emb_done"], 2 + j + 1 + i * RING)
                    for w in range(DH):
                        ins = pe.matmul(bank[(0, 1, 6, 7)[j % EB]][:, w * P:w * P + P], emb[:, j % EB, w * P:w * P + P],
                                        hot[:, j % HOT, :], start=True, stop=True)
                    ins.then_inc(S["e_mm"], 1)

                def ring_of_products(i, last):
                    for j in range(RING):
                        for ahead, part in ((2, turn_attributes), (1, first_linear), (0, products)):
                            if not last or j + ahead < RING:
                                part(i + (j + ahead) // RING, (j + ahead) % RING)

                turn_attributes(0, 0)
                turn_attributes(0, 1)
                first_linear(0, 0)
                tiles_in_order(pe, ring_of_products)

            first_rows_to_columns()
            pe.wait_ge(S["w_in"], 16 * (1 + 2 * L + 3))
            linear(0, W_in, 2, ("ev_T", 4, 4))
            columns_to_rows(0)
            pe.wait_ge(S["ev_T"], 4 * NG + 3 * NG)
            edge_embeddings()
            pe.wait_ge(S["e_summed"], 1)
            for l in range(L):
                one_hot_products(l)
                pe.wait_ge(S["acc_done"], NT * (l + 1) + AC)
                linear(first_linear_of(l), W1[:, l, :, :], 0)
                linear(first_linear_of(l) + 1, W2[:, l, :, :], 2, ("app_done", 4 * NG * l + 2, 2))
                columns_to_rows(l + 1)
                if l == 0:
                    pe.wait_ge(S["e2_in"], 16)
                    linear(SUMS, ee2, 2)
                    pe.wait_ge(S["ev_done"], 4 + 4 * NG * (SUMS + 1))
            last_rows_to_columns()
            pe.wait_ge(S["ev_T"], 8 * NG + 3 * NG * AG)
            one_hot_products(AG - 1)
            pe.wait_ge(S["wl1_in"], 16 * (DH + KH + 1))

            def first_map(b):
                pe.wait_ge(S["m_blk"], 2 + b * 2)
                for q in range(2):
                    for kk in range(DH):
                        ins = pe.matmul(bank[q][:, :], hblk[:, kk, :], w1[:, kk, q * 512:q * 512 + 512],
                                        start=kk == 0, stop=kk == DH - 1)
                ins.then_inc(S["m_mm1"], 1)

            def turn(s, b):
                pe.wait_ge(S[("m_nz1", "m_nz2")[s]], 1 + b)
                if s == 0 and (not isinstance(b, int) or b >= 2):
                    pe.wait_ge(S["m_a2"], b * KH - KH)
                if s == 1 and (not isinstance(b, int) or b < NB - 1):
                    pe.wait_ge(S["m_a1"], b * KH + 2 * KH)
                for kk in range(KH):
                    ins = pe.transpose(bank[2 + kk // 4][:, kk % 4 * P:kk % 4 * P + P], z[s][:, kk * P:kk * P + P],
                                       ident[:, :])
                    if kk % 4 == 3:
                        ins.then_inc(S[("m_t1", "m_t2")[s]], 1)

            def second_map(b):
                for q in range(2):
                    for kk in range(KH):
                        pe.wait_ge(S["m_a1"], kk + 1 + b * KH)
                        ins = pe.matmul(bank[4 + q][:, :], zT[0][:, kk, :], w2[:, kk, q * 512:q * 512 + 512],
                                        start=kk == 0, stop=kk == KH - 1)
                ins.then_inc(S["m_mm2"], 1)

            def third_map(b):
                pe.wait_ge(S["m_y"], YC - 7 + b * 8)
                for kk in range(KH):
                    pe.wait_ge(S["m_a2"], kk + 1 + b * KH)
                    ins = pe.matmul(bank[6][:, 0:D], zT[1][:, kk, :], w3[:, kk, :], start=kk == 0, stop=kk == KH - 1)
                ins.then_inc(S["m_mm3"], 1)

            skewed(pe, ((1, first_map), (-2, third_map), (-1, lambda b: turn(1, b)), (0, second_map),
                        (1, lambda b: turn(0, b))))


_INS = ['x', 'src', 'dst', 'edge_attr_64', 'edge_weight', 'L0_gnn_W_in', 'L0_gnn_b_in', 'L0_gnn_W1', 'L0_gnn_b1',
        'L0_gnn_g1', 'L0_gnn_be1', 'L0_gnn_W2', 'L0_gnn_b2', 'L0_gnn_g_out', 'L0_gnn_b_out', 'L1_gnn_eps',
        'L1_gnn_ee_w1', 'L1_gnn_ee_b1', 'L1_gnn_ee_w2', 'L1_gnn_ee_b2', 'L1_gnn_w1', 'L1_gnn_b1', 'L1_gnn_g1',
        'L1_gnn_be1', 'L1_gnn_w2', 'L1_gnn_b2', 'L1_gnn_g2', 'L1_gnn_be2', 'L1_gnn_w3', 'L1_gnn_b3', 'L1_gnn_bn_g',
        'L1_gnn_bn_b']


def kernel(**inputs):
    import numpy as np
    import concourse.bacc as bacc
    from concourse.bass_utils import run_bass_kernel_spmd as run

    nc = bacc.Bacc("TRN2", target_bir_lowering=False, num_devices=1)
    arrays, tensors = {}, {}
    for name in _INS:
        a = np.ascontiguousarray(inputs[name])
        if a.ndim == 0:
            a = a.reshape(1)
        arrays[f"in_{name}"] = a
        tensors[name] = nc.dram_tensor(f"in_{name}", a.shape, mybir.dt.from_np(a.dtype), kind="ExternalInput").ap()
    out = nc.dram_tensor("out_0", (N, D), F32, kind="ExternalOutput").ap()
    build(nc, tensors, out)
    r = run(nc, [arrays], core_ids=[0])
    return r.results[0]["out_0"]
```
